# Optimizing a Trainium2 kernel written in Bass

```python
import numpy as np
import jax
import jax.numpy as jnp

def _softmax(x, axis=-1):
    return jax.nn.softmax(x, axis=axis)
def _gelu(x):
    return jax.nn.gelu(x, approximate=True)
def _silu(x):
    return jax.nn.silu(x)
def _sigmoid(x):
    return jax.nn.sigmoid(x)
def _layernorm(x, axis=-1, eps=1e-5):
    m = jnp.mean(x, axis=axis, keepdims=True)
    v = jnp.var(x, axis=axis, keepdims=True)
    return (x - m) / jnp.sqrt(v + eps)
def _scatter_add(tgt, idx, src, axis=0):
    return tgt.at[idx].add(src)
def _segment_sum(src, seg, n):
    return jax.ops.segment_sum(src, seg, n)

kernel_name = 'mk_adj_resnorm_d2_adj_128_193c48'

def setup_inputs(seed: int = 0):
    np.random.seed(seed)
    _w = jnp.asarray
    def _rec_inputs():
        import jax
        import jax.numpy as jnp
        _gk = jax.random.key(seed)
        x = -0.000929 + 1 * jax.random.normal(jax.random.fold_in(_gk, 1), (8192, 128), jnp.float32)
        _a = jax.random.bernoulli(jax.random.fold_in(_gk, 2), 0.000488281, (8192, 8192))
        _a = jnp.logical_or(_a, jnp.eye(8192, dtype=bool))
        _af = _a.astype(jnp.float32)
        _af = _af * jax.random.uniform(jax.random.fold_in(_gk, 3), (8192, 8192), jnp.float32, 0.05, 1)
        adj = _af
        return x, adj
    x, adj = _rec_inputs()
    def _L0_gnn_setup():
        import jax, jax.numpy as jnp
        import numpy as np
        N = 8192
        H = 128
        key = jax.random.key(seed)
        k_x, k_A, k_W = jax.random.split(key, 3)
        x = jax.random.normal(k_x, (N, H), dtype=jnp.float32)
        A = jax.random.uniform(k_A, (N, N), dtype=jnp.float32)
        alpha = jnp.array([0.5], dtype=jnp.float32)
        bound = 1.0 / np.sqrt(H)
        W = jax.random.uniform(k_W, (H, H), dtype=jnp.float32, minval=-bound, maxval=bound)
        b = jnp.zeros((H,), dtype=jnp.float32)
        t = jnp.zeros((1,), dtype=jnp.float32)
        return {'t': t, 'x': x, 'A': A, 'alpha': alpha, 'W': W, 'b': b}
    _L0_gnn_all = _L0_gnn_setup()
    _L0_gnn_in = {k: v for k, v in _L0_gnn_all.items() if k in ('t', 'alpha', 'W', 'b', )}
    del _L0_gnn_all

    def _L1_gnn_setup():
        import jax, jax.numpy as jnp
        import numpy as np

        def _lap_mul(A, x):
            d = 1.0 / jnp.sqrt(jnp.sum(A, axis=-1))
            return d[:, None] * (A @ (d[:, None] * x))
        key = jax.random.key(seed)
        k1, k2, k3, k4, k5, k6 = jax.random.split(key, 6)
        N, D_IN, D_OUT = (4096, 128, 128)
        x = jax.random.normal(k1, (N, D_IN), dtype=jnp.float32)
        A = jax.random.uniform(k2, (N, N), dtype=jnp.float32)
        s1 = 1.0 / np.sqrt(D_IN)
        W1 = jax.random.uniform(k3, (D_IN, D_OUT), minval=-s1, maxval=s1, dtype=jnp.float32)
        b1 = jax.random.uniform(k4, (D_OUT,), minval=-s1, maxval=s1, dtype=jnp.float32)
        W2 = jax.random.uniform(k5, (D_IN, D_OUT), minval=-s1, maxval=s1, dtype=jnp.float32)
        b2 = jax.random.uniform(k6, (D_OUT,), minval=-s1, maxval=s1, dtype=jnp.float32)
        return {'x': x, 'A': A, 'W1': W1, 'b1': b1, 'W2': W2, 'b2': b2, 'sigma': 1, 'k': 4}
    _L1_gnn_all = _L1_gnn_setup()
    _L1_gnn_in = {k: v for k, v in _L1_gnn_all.items() if k in ('W1', 'b1', 'W2', 'b2', )}
    del _L1_gnn_all

    return {
        "x": x,
        "adj": adj,
        "L0_gnn_t": _L0_gnn_in["t"],
        "L0_gnn_alpha": _L0_gnn_in["alpha"],
        "L0_gnn_W": _L0_gnn_in["W"],
        "L0_gnn_b": _L0_gnn_in["b"],
        "L1_gnn_W1": _L1_gnn_in["W1"],
        "L1_gnn_b1": _L1_gnn_in["b1"],
        "L1_gnn_W2": _L1_gnn_in["W2"],
        "L1_gnn_b2": _L1_gnn_in["b2"],
    }

def reference(x, adj, L0_gnn_t, L0_gnn_alpha, L0_gnn_W, L0_gnn_b, L1_gnn_W1, L1_gnn_b1, L1_gnn_W2, L1_gnn_b2):
    import jax
    import jax.numpy as jnp
    def _L0_gnn_ref(t, x, A, alpha, W, b):
        import jax, jax.numpy as jnp
        import numpy as np
        N = 8192
        H = 128
        a = alpha[0]
        A_prime = a * A
        diag = jnp.diagonal(A_prime) + (1.0 - a)
        A_prime = A_prime.at[jnp.arange(N), jnp.arange(N)].set(diag)
        out_degree = A_prime.sum(axis=1)
        inv_deg = jnp.where(out_degree == 0.0, 0.0, 1.0 / out_degree)
        x = inv_deg[:, None] * A_prime @ x
        x = x @ W.T + b
        return jax.nn.relu(x)

    def _L1_gnn_ref(x, A, W1, b1, W2, b2, sigma, k):
        import jax, jax.numpy as jnp
        import numpy as np

        def _lap_mul(A, x):
            d = 1.0 / jnp.sqrt(jnp.sum(A, axis=-1))
            return d[:, None] * (A @ (d[:, None] * x))
        z = _lap_mul(A, x) @ W1 + b1
        z = jax.nn.leaky_relu(z, negative_slope=0.1)
        sq = jnp.sum(z * z, axis=-1)
        d2 = sq[:, None] + sq[None, :] - 2.0 * (z @ z.T)
        d2 = jnp.maximum(d2, 0.0)
        S = jnp.sqrt(d2 + 1e-10)
        S = jnp.exp(-S / (2.0 * sigma))
        order = jnp.argsort(-S, axis=-1)
        ranks = jnp.argsort(order, axis=-1)
        S = jnp.where(ranks < k, S, 0.0)
        A2 = S + A
        out = _lap_mul(A2, x) @ W2 + b2
        return out

    x = _layernorm(x + _L0_gnn_ref(L0_gnn_t, x, adj, L0_gnn_alpha, L0_gnn_W, L0_gnn_b), axis=-1)
    x = _layernorm(x + _L1_gnn_ref(x, adj, L1_gnn_W1, L1_gnn_b1, L1_gnn_W2, L1_gnn_b2, 1, 4), axis=-1)
    return x


_drawn_inputs = setup_inputs


def setup_inputs(seed=0):
    import zlib

    import numpy as np

    out = dict(_drawn_inputs(seed))
    spreads = {'L0_gnn_b': (0.0, 0.1)}
    factors = {}
    for name, (base, spread) in spreads.items():
        noise = np.random.default_rng([zlib.crc32(name.encode()), seed]).standard_normal(out[name].shape)
        drawn = base * np.exp(spread * noise) if base else spread * noise
        out[name] = jnp.asarray(drawn.astype(out[name].dtype))
    for name, factor in factors.items():
        out[name] = (out[name] * factor).astype(out[name].dtype)
    return out
```

```python
from contextlib import ExitStack

import concourse.bass as bass
from concourse import mybir


def bass_adj_resnorm_d2(nc: bass.Bass, x: bass.AP, adj: bass.AP, t0: bass.AP, alpha: bass.AP,
                        w0: bass.AP, b0: bass.AP, w1: bass.AP, b1: bass.AP, w2: bass.AP, b2: bass.AP,
                        out: bass.AP):
    f32, f32r, u32 = mybir.dt.float32, mybir.dt.float32r, mybir.dt.uint32
    ALU, ACT, AX = mybir.AluOpType, mybir.ActivationFunctionType, mybir.AxisListType

    P = 128
    N, F = x.shape
    NT = N // P
    IB = 512
    TI = IB // P
    NB = N // IB
    NP = NT // 2
    CW = 512
    NC = N // CW
    SLOTS = 4
    SPLITS = 4
    K = 4
    JW = 1024
    JC = N // JW
    XP = 4
    EPS = 1e-5
    STEPS = NB * NP

    EPI = [30, 6, 24]
    NORM_AT = [12, None, 6]
    EPI_BASE = [0, NB * EPI[0], NB * (EPI[0] + EPI[1])]
    V_BASE = [0, NT, 2 * NT + JC]
    TERM_P = NP - 2
    EPI_P = [[min(2 + n * 20 // EPI[phase] * NP // 32, NP - 1) for n in range(EPI[phase])] for phase in range(3)]
    SUM_P = [(2 + 7 * (m // K) + m % K) * NP // 32 for m in range(TI * K)]
    SQUARE_P = 24 * NP // 32
    ZT_P = 26 * NP // 32

    x1_dram = nc.dram_tensor("x1_scratch", (N, F), f32, kind="Internal").ap()
    v3_dram = nc.dram_tensor("v3_scratch", (N, F), f32, kind="Internal").ap()
    sq_dram = nc.dram_tensor("sq_scratch", (2, N), f32, kind="Internal").ap()

    def rows(t, b):
        return t[bass.ds(b * IB, IB), :].rearrange("(t p) n -> p t n", p=P)

    def wait(eng, sem, value):
        if not (isinstance(value, int) and value <= 0):
            eng.wait_ge(sem, value)

    def wait_apart(eng, *waits):
        for sem, v in waits:
            if not (isinstance(v, int) and v <= 0):
                eng.wait_ge(sem, v).then_inc(passed[eng], 1)

    def epi_at(phase, b, n):
        return b * EPI[phase] + (EPI_BASE[phase] + n)

    ctx = ExitStack()
    with ctx:
        def sb(name, shape, dt):
            return ctx.enter_context(nc.sbuf_tensor(name, shape, dt))

        def pb(name, shape, dt):
            return ctx.enter_context(nc.psum_tensor(name, shape, dt))

        def sem(name):
            return ctx.enter_context(nc.semaphore(name))

        a_nat = [sb(f"a_nat{s}", [P, TI, CW], f32) for s in range(SLOTS)]
        a_hi = [sb(f"a_hi{s}", [P, 2, IB], f32r) for s in range(SPLITS)]
        a_lo = [sb(f"a_lo{s}", [P, 2, IB], f32r) for s in range(SPLITS)]
        v_hi = sb("v_hi", [P, NT, P], f32r)
        v_lo = sb("v_lo", [P, NT, P], f32r)
        z_hi = v_hi[:, :, :].rearrange("p t n -> p (t n)")
        z_lo = v_lo[:, :, :].rearrange("p t n -> p (t n)")
        big = [sb(f"big{s}", [P, NT, P], f32) for s in range(2)]
        bigw = [t[:, :, :].rearrange("p t n -> p (t n)") for t in big]
        u_sb = sb("u_sb", [P, IB], f32)
        term = sb("term", [P, TI, P], f32)
        y = sb("y", [P, TI, P], f32)
        ident = sb("ident", [P, P], f32)
        consts = sb("consts", [P, 7, P], f32)
        one_less = consts[:, 4, :]
        w0_nat = y[:, 0, :]
        w_sb = [consts[:, n, :] for n in (0, 2, 5)]
        b_sb = [consts[:, n, :] for n in (1, 3, 6)]
        al = sb("al", [P, 1], f32)
        oma = sb("oma", [P, 1], f32)
        rparts = sb("rparts", [P, TI, NC], f32)
        rs4 = sb("rs4", [P, TI], f32)
        deg4 = sb("deg4", [P, TI], f32)
        mask4 = sb("mask4", [P, TI], f32)
        safe4 = sb("safe4", [P, TI], f32)
        rec4 = sb("rec4", [P, TI], f32)
        inv4 = sb("inv4", [P, TI], f32)
        d4 = sb("d4", [P, TI], f32)
        stats = sb("stats", [P, TI, 6], f32)
        aggr = sb("aggr", [P, TI, 2], f32)
        rstd = sb("rstd", [P, TI], f32)
        ve = sb("ve", [P, TI], f32)
        std4 = sb("std4", [P, TI], f32)
        tmp4 = sb("tmp4", [P, TI], f32)
        root = y[:, 0:TI // 2, :].rearrange("p t n -> p (t n)")[:, 0:NT * K]
        tmp = y[:, TI // 2:TI, :].rearrange("p t n -> p (t n)")[:, 0:NT * K]
        rsum = sb("rsum", [P, NT], f32)
        d_all = sb("d_all", [P, NT], f32)
        sq4 = sb("sq4", [P, TI], f32)
        sq_all = sb("sq_all", [P, P], f32)
        PB = 2 * IB // P
        picks = [a_hi[2 + h][:, :, :].rearrange("p a (b n) -> p (a b) n", n=P) for h in range(NB // PB)]
        pick = [picks[n // PB][:, n % PB, :] for n in range(NB)]
        zi_hi = [a_lo[2][:, 0, s * P:(s + 1) * P] for s in range(2)]
        zi_lo = [a_lo[2][:, 1, s * P:(s + 1) * P] for s in range(2)]
        sq_hi, sq_lo = a_lo[3][:, 0, 0:P], a_lo[3][:, 0, P:2 * P]
        sq_rows = a_lo[3][:, 1, :]
        m8 = [sb(f"m8_{s}", [P, 8], f32) for s in range(2)]
        i8 = [sb(f"i8_{s}", [P, 8], u32) for s in range(2)]
        val = u_sb[:, 0:NT * K].rearrange("p (t k) -> p t k", k=K)
        idx = consts[:, 2:4, :].rearrange("p a n -> p (a n)").bitcast(u32)[:, 0:NT * K].rearrange("p (t k) -> p t k", k=K)
        dist = u_sb[:, IB // 2:IB // 2 + NT * K].rearrange("p (t k) -> p t k", k=K)
        s_w = consts[:, 0:2, :].rearrange("p a n -> p (a n)")[:, 0:NT * K].rearrange("p (t k) -> p t k", k=K)
        ssum = sb("ssum", [P, NT], f32)
        idx16 = sb("idx16", [P, TI * K], u32)
        s16 = sb("s16", [P, TI * K], f32)
        got = sb("got", [P, K, P], f32)

        t_ps = [pb(f"t_ps{s}", [P, 2, IB], f32) for s in range(2)]
        acc = pb("acc", [P, IB], f32)
        h_ps = pb("h_ps", [P, TI, P], f32)
        zt_ps = pb("zt_ps", [P, IB], f32)
        junk = pb("junk", [P, CW], f32)

        a_in = [sem(f"a_in{s}") for s in range(SLOTS)]
        const_in, x_in, rows_out = sem("const_in"), sem("x_in"), sem("rows_out")
        xn_in = [sem(f"xn_in{s}") for s in range(XP)]
        made, picked, w0_t, w0_done = sem("made"), sem("picked"), sem("w0_t"), sem("w0_done")
        tr_done, hi_done, lo_done, mm_done = sem("tr_done"), sem("hi_done"), sem("lo_done"), sem("mm_done")
        rs_act, rs_dve = sem("rs_act"), sem("rs_dve")
        u_done, h_done, epi, term_done = sem("u_done"), sem("h_done"), sem("epi"), sem("term_done")
        vhi_done, vlo_done = sem("vhi_done"), sem("vlo_done")
        zt_done, zt_saved, sq_done, sq_saved = sem("zt_done"), sem("zt_saved"), sem("sq_done"), sem("sq_saved")
        d_done, sqt_done, sqh_done, sql_done, sq_out, sq_in = (
            sem("d_done"), sem("sqt_done"), sem("sqh_done"), sem("sql_done"), sem("sq_out"), sem("sq_in"))
        zi_done, gr_done, sc_done, topk, vi_saved = (
            sem("zi_done"), sem("gr_done"), sem("sc_done"), sem("topk"), sem("vi_saved"))
        wt, exp_done, v3_done, v3_out, staged = (
            sem("wt"), sem("exp_done"), sem("v3_done"), sem("v3_out"), sem("staged"))
        got_in = sem("got_in")
        s_done = sem("s_done")
        dmy, std_done, root_done, chain = sem("dmy"), sem("std_done"), sem("root_done"), sem("chain")

        block = ctx.enter_context(nc.Block())

        CONSTS = 16 * 7
        dve_passed, pool_passed = sem("dve_passed"), sem("pool_passed")
        passed = {}

        @block.sync
        def _(sp):
            def load_a(phase, b, c):
                before = b * NP + (phase * STEPS + 2 * (c - SLOTS) + 2)
                wait(sp, tr_done, before)
                if phase == 0 or (phase == 1 and isinstance(b, int) and c < SLOTS):
                    wait(sp, rs_act, before)
                    wait(sp, rs_dve, before)
                sp.dma_start(a_nat[c % SLOTS][:, :, :],
                             rows(adj, b)[:, :, c * CW:(c + 1) * CW]).then_inc(a_in[c % SLOTS], 16)

            def load_x(b):
                wait(sp, term_done, b)
                if not (isinstance(b, int) and b == 0):
                    sp.wait_ge(epi, epi_at(0, b - 1, 12))
                sp.dma_start(term[:, :, :], rows(x, b)).then_inc(x_in, 16)

            def save_x1(b):
                sp.wait_ge(epi, epi_at(0, b, EPI[0]))
                sp.dma_start(rows(x1_dram, b), big[0][:, bass.ds(b * TI, TI), :]).then_inc(rows_out, 16)

            def save_out(b):
                sp.wait_ge(epi, epi_at(2, b, EPI[2]))
                sp.dma_start(rows(out, b), y[:, :, :]).then_inc(rows_out, 16)

            load_a(0, 0, 0)
            sp.dma_start(al[:, :], alpha.partition_broadcast(P)).then_inc(const_in, 16)
            for n in range(XP):
                w = NT // XP
                sp.dma_start(big[0][:, n * w:(n + 1) * w, :],
                             x[n * w * P:(n + 1) * w * P, :].rearrange("(t p) d -> p t d", p=P)).then_inc(xn_in[n], 16)
                if n + 1 < SLOTS:
                    load_a(0, 0, n + 1)
            sp.dma_start(w0_nat, w0).then_inc(const_in, 16)
            for n, w in ((1, w1), (2, w2)):
                sp.dma_start(w_sb[n][:, :], w).then_inc(const_in, 16)
            for n, b in enumerate((b0, b1, b2)):
                sp.dma_start(b_sb[n][:, :], b.partition_broadcast(P)).then_inc(const_in, 16)
            load_x(0)
            for c in range(SLOTS, NC):
                load_a(0, 0, c)
            with sp.Fori(1, NB) as b:
                for c in range(NC):
                    load_a(0, b, c)
                    if c == NC // 2:
                        load_x(b)
                    if c == NC - 1:
                        save_x1(b - 1)
            for c in range(SLOTS):
                load_a(1, 0, c)
            save_x1(NB - 1)
            for c in range(SLOTS, NC):
                load_a(1, 0, c)
            with sp.Fori(1, NB) as b:
                for c in range(NC):
                    load_a(1, b, c)
            for c in range(SLOTS + 1):
                load_a(2, 0, c)
            sp.wait_ge(sqh_done, 1)
            sp.dma_start(sq_dram[0, :].rearrange("(t p) -> t p", p=P), sq_hi[0:NT, :].bitcast(f32)).then_inc(sq_out, 16)
            sp.wait_ge(sql_done, 1)
            sp.dma_start(sq_dram[1, :].rearrange("(t p) -> t p", p=P), sq_lo[0:NT, :].bitcast(f32)).then_inc(sq_out, 16)
            sp.wait_ge(sq_out, 32)
            sp.wait_ge(picked, 1)
            sp.dma_start(sq_rows[0:2 * NB, :].bitcast(f32), sq_dram.rearrange("h (b n) -> (h b) n", n=IB)).then_inc(sq_in, 16)
            sp.wait_ge(rows_out, 16 * NB)
            sp.wait_ge(topk, 2 * (NT - 1))
            for n in range(XP):
                w = NT // XP
                sp.dma_start(big[0][:, n * w:(n + 1) * w, :],
                             x1_dram[n * w * P:(n + 1) * w * P, :].rearrange("(t p) d -> p t d", p=P)).then_inc(xn_in[n], 16)
            for c in range(SLOTS + 1, NC):
                load_a(2, 0, c)
            with sp.Fori(1, NB) as b:
                for c in range(NC):
                    load_a(2, b, c)
                    if c == NC - 1:
                        save_out(b - 1)
            save_out(NB - 1)
            sp.wait_ge(rows_out, 32 * NB)

        @block.gpsimd
        def _(pool):
            passed[pool] = pool_passed
            nc.gpsimd.memset(ident[:, :], 0.0).then_inc(made, 1)
            nc.gpsimd.memset(sq_all[:, :], 0.0).then_inc(sq_saved, 1)
            pool.wait_ge(sq_saved, 1)
            pool.wait_ge(made, 1)
            nc.gpsimd.affine_select(out=ident[:, :], in_=ident[:, :], compare_op=ALU.not_equal, fill=1.0, base=0,
                                    pattern=[[-1, P]], channel_multiplier=1).then_inc(made, 1)

            def save_sq(b):
                pool.wait_ge(sq_done, TI * b + TI)
                nc.gpsimd.tensor_copy(sq_all[:, bass.ds(b * TI, TI)], sq4[:, :]).then_inc(sq_saved, 1)

            save_sq(0)
            with pool.Fori(1, NB) as b:
                save_sq(b)

            pool.wait_ge(mm_done, 2 * STEPS)
            nc.gpsimd.memset(sq_rows.bitcast(f32), 0.0).then_inc(picked, 1)
            for h in range(NB // PB):
                nc.gpsimd.memset(picks[h].bitcast(f32), 0.0).then_inc(picked, 1)
            for row in range(2):
                pool.wait_ge(picked, 1 + NB // PB * (1 + row))
                for h in range(NB // PB):
                    nc.gpsimd.affine_select(out=picks[h], in_=picks[h], compare_op=ALU.not_equal, fill=1.0,
                                            base=-row * NB - h * PB, pattern=[[-1, PB], [0, P]],
                                            channel_multiplier=1).then_inc(picked, 1)

            def stage(i, s):
                wait(pool, gr_done, i * JC - JC)
                nc.gpsimd.tensor_copy(zi_hi[s], z_hi[:, bass.ds(i * P, P)]).then_inc(zi_done, 1)
                nc.gpsimd.tensor_copy(zi_lo[s], z_lo[:, bass.ds(i * P, P)]).then_inc(zi_done, 1)

            def save_best(i, s):
                pool.wait_ge(topk, i * 2 + 2)
                nc.gpsimd.tensor_copy(val[:, bass.ds(i, 1), :].rearrange("p a k -> p (a k)"), m8[s][:, 0:K]).then_inc(vi_saved, 1)
                nc.gpsimd.tensor_copy(idx[:, bass.ds(i, 1), :].rearrange("p a k -> p (a k)"), i8[s][:, 0:K]).then_inc(vi_saved, 1)

            pool.wait_ge(vlo_done, 2 * NT + JC)
            stage(0, 0)
            stage(1, 1)
            save_best(0, 0)
            with pool.Fori(2, NT - 1, 2) as i:
                stage(i, 0)
                save_best(i - 1, 1)
                stage(i + 1, 1)
                save_best(i, 0)
            save_best(NT - 1, 1)

            pool.wait_ge(d_done, 2)
            for n in range(XP):
                w = NT // XP
                pool.wait_ge(xn_in[n], 32)
                for t in range(n * w, (n + 1) * w):
                    nc.gpsimd.tensor_scalar(big[1][:, t, :], big[0][:, t, :], d_all[:, t:t + 1], None,
                                            ALU.mult).then_inc(v3_done, 1)
                pool.wait_ge(v3_done, (n + 1) * w)
                pool.dma_start(v3_dram[n * w * P:(n + 1) * w * P, :].rearrange("(t p) d -> p t d", p=P),
                               big[1][:, n * w:(n + 1) * w, :]).then_inc(v3_out, 16)
            pool.wait_ge(v3_out, 16 * XP)
            pool.wait_ge(exp_done, 1)

            def gather(b):
                wait(pool, s_done, b * (TI * K))
                nc.gpsimd.tensor_copy(idx16[:, :].rearrange("p (t k) -> p t k", k=K),
                                      idx[:, bass.ds(b * TI, TI), :]).then_inc(staged, 1)
                nc.gpsimd.tensor_copy(s16[:, :].rearrange("p (t k) -> p t k", k=K),
                                      s_w[:, bass.ds(b * TI, TI), :]).then_inc(staged, 1)
                wait_apart(pool, (staged, b * 2 + 2))
                for t in range(TI):
                    if t > 0:
                        wait_apart(pool, (s_done, b * (TI * K) + t * K))
                    for k in range(K):
                        n = t * K + k
                        nc.gpsimd.indirect_dma_start(
                            out=got[:, k, :], out_offset=None, in_=v3_dram[:, :],
                            in_offset=bass.IndirectOffsetOnAxis(ap=idx16[:, n:n + 1], axis=0)).then_inc(got_in, 16)

            gather(0)
            with pool.Fori(1, NB) as b:
                gather(b)

        @block.scalar
        def _(act):
            def split_v(phase, t):
                src = big[0][:, t, :]
                if phase != 1 and t % (NT // XP) == 0:
                    act.wait_ge(xn_in[t // (NT // XP)], 16 if phase == 0 else 32)
                if t == 0 and phase == 0:
                    act.wait_ge(const_in, CONSTS)
                if t == 0 and phase > 0:
                    act.wait_ge(d_done, phase)
                scale = al[:, 0:1] if phase == 0 else d_all[:, t:t + 1]
                nc.scalar.activation(v_hi[:, t, :], src, ACT.Copy, scale=scale).then_inc(vhi_done, 1)

            def evac_hi(phase, b, q):
                at = b * NP + (phase * STEPS + q)
                act.wait_ge(tr_done, at + 1)
                wait(act, mm_done, at - (SPLITS - 1))
                nc.scalar.activation(a_hi[q % SPLITS][:, :, :], t_ps[q % 2][:, :, :], ACT.Copy).then_inc(hi_done, 1)

            def save_u(phase, b):
                act.wait_ge(mm_done, b * NP + (phase * STEPS + NP))
                nc.scalar.activation(u_sb[:, :], acc[:, :], ACT.Copy).then_inc(u_done, 1)

            def square(b):
                act.wait_ge(epi, epi_at(1, b, EPI[1]))
                act.wait_ge(sq_saved, b + 1)
                for t in range(TI):
                    nc.scalar.activation(junk[:, t * P:(t + 1) * P], y[:, t, :], ACT.Square, accum_out=sq4[:, t:t + 1]).then_inc(sq_done, 1)

            def find_std(phase, b):
                act.wait_ge(epi, epi_at(phase, b, NORM_AT[phase] + 9))
                nc.scalar.activation(std4[:, :], ve[:, :], ACT.Sqrt).then_inc(std_done, 1)

            def find_root(ready, count, to, v):
                act.wait_ge(ready, count)
                nc.scalar.activation(to, v, ACT.Sqrt).then_inc(root_done, 1)

            def save_zt(b):
                act.wait_ge(zt_done, b + 1)
                nc.scalar.activation(bigw[1][:, bass.ds(b * IB, IB)], zt_ps[:, :], ACT.Copy).then_inc(zt_saved, 1)

            def row_sum(b, p):
                if p == 0:
                    if not (isinstance(b, int) and b == 0):
                        act.wait_ge(epi, epi_at(0, b - 1, 1))
                wait(act, rs_act, b * NP + p)
                nc.scalar.activation(junk[:, :], a_nat[(p // 2) % SLOTS][:, p % 2, :], ACT.Copy,
                                     accum_out=rparts[:, p % 2, p // 2:p // 2 + 1]).then_inc(rs_act, 1)

            def one_block(phase, b, first=False, last=False):
                if not first:
                    save_u(phase, b - 1)
                for p in range(NP):
                    if first:
                        split_v(phase, 2 * p)
                        split_v(phase, 2 * p + 1)
                    if not (last and p + 2 >= NP):
                        evac_hi(phase, b, p + 2)
                    if phase == 0:
                        row_sum(b, p)
                    if phase != 1 and not first and p == EPI_P[phase][NORM_AT[phase] + 8] + 1:
                        find_std(phase, b - 1)
                    if phase == 1 and not first:
                        if p == SQUARE_P:
                            square(b - 1)
                        if p == ZT_P + 1:
                            save_zt(b - 1)

            act.wait_ge(w0_t, 1)
            nc.scalar.activation(w_sb[0][:, :], h_ps[:, 0, :], ACT.Copy).then_inc(w0_done, 1)
            evac_hi(0, 0, 0)
            evac_hi(0, 0, 1)
            one_block(0, 0, first=True)
            with act.Fori(1, NB) as b:
                one_block(0, b)
            save_u(0, NB - 1)
            find_std(0, NB - 1)
            find_root(epi, epi_at(0, NB, 0), root[:, 0:NT], rsum[:, :])
            one_block(1, 0, first=True)
            with act.Fori(1, NB) as b:
                one_block(1, b)
            save_u(1, NB - 1)
            square(NB - 1)
            save_zt(NB - 1)
            act.wait_ge(zt_saved, NB)
            for c in range(JC):
                nc.scalar.activation(z_hi[:, c * JW:(c + 1) * JW], bigw[1][:, c * JW:(c + 1) * JW], ACT.Copy).then_inc(vhi_done, 1)
                if c == 0:
                    act.wait_ge(sqt_done, 1)
                    nc.scalar.activation(sq_hi, h_ps[:, 0, :], ACT.Copy, scale=-0.5).then_inc(sqh_done, 1)

            def evac_scores(i, s):
                for c in range(JC):
                    act.wait_ge(gr_done, i * JC + (c + 1))
                    if c == 0:
                        wait(act, topk, 2 * i - 2)
                    nc.scalar.activation(bigw[s][:, c * JW:(c + 1) * JW],
                                         t_ps[c % 2][:, :, :].rearrange("p a n -> p (a n)"), ACT.Copy).then_inc(sc_done, 1)

            act.wait_ge(vlo_done, 2 * NT + JC)
            evac_scores(0, 0)
            evac_scores(1, 1)
            with act.Fori(2, NT - 1, 2) as i:
                evac_scores(i, 0)
                evac_scores(i + 1, 1)
            find_root(wt, 2, root, dist[:, :, :].rearrange("p t k -> p (t k)"))
            act.wait_ge(wt, 4)
            nc.scalar.activation(s_w[:, :, :], dist[:, :, :], ACT.Exp, scale=-0.5).then_inc(exp_done, 1)
            find_root(wt, 6, root[:, 0:NT], rsum[:, :])
            one_block(2, 0, first=True)
            with act.Fori(1, NB - 1) as b:
                one_block(2, b)
            one_block(2, NB - 1, last=True)
            save_u(2, NB - 1)
            find_std(2, NB - 1)

        @block.vector
        def _(dve):
            passed[dve] = dve_passed
            def split_v(phase, t):
                dve.wait_ge(vhi_done, V_BASE[phase] + t + 1)
                scale = al[:, 0:1] if phase == 0 else d_all[:, t:t + 1]
                nc.vector.scalar_tensor_tensor(v_lo[:, t, :], big[0][:, t, :], scale, v_hi[:, t, :],
                                               ALU.mult, ALU.subtract).then_inc(vlo_done, 1)

            def evac_lo(phase, b, q):
                dve.wait_ge(hi_done, b * NP + (phase * STEPS + q + 1))
                nc.vector.tensor_tensor(a_lo[q % SPLITS][:, :, :], t_ps[q % 2][:, :, :],
                                        a_hi[q % SPLITS][:, :, :], ALU.subtract).then_inc(lo_done, 1)

            def row_sum(b, p):
                if p == 0 and not (isinstance(b, int) and b == 0):
                    dve.wait_ge(epi, epi_at(0, b - 1, 1))
                nc.vector.tensor_reduce(rparts[:, 2 + p % 2, p // 2:p // 2 + 1], a_nat[(p // 2) % SLOTS][:, 2 + p % 2, :],
                                        AX.X, ALU.add).then_inc(rs_dve, 1)

            def newton(k, to, r, v, tmp):
                if k == 0:
                    return nc.vector.tensor_tensor(tmp, r, r, ALU.mult)
                if k == 1:
                    return nc.vector.tensor_tensor(tmp, tmp, v, ALU.mult)
                if k == 2:
                    return nc.vector.tensor_scalar(tmp, tmp, -0.5, 1.5, ALU.mult, ALU.add)
                return nc.vector.tensor_tensor(to, r, tmp, ALU.mult)

            def inverse_root(call, to, v, r, tmp):
                dve.wait_ge(root_done, call + 1)
                nc.vector.reciprocal(r, r).then_inc(chain, 1)
                for k in range(3):
                    dve.wait_ge(chain, 4 * call + k + 1)
                    newton(k, to, r, v, tmp).then_inc(chain, 1)
                dve.wait_ge(chain, 4 * call + 4)
                return newton(3, to, r, v, tmp)

            def norm(phase, b, n, at, dst):
                k = n - at
                if k < 4:
                    dve.wait_ge(epi, epi_at(phase, b, at))
                    nc.vector.bn_stats(stats[:, k, :], y[:, k, :]).then_inc(epi, 1)
                elif k < 8:
                    if k == 4:
                        wait_apart(dve, (epi, epi_at(phase, b, at + 4)))
                    nc.vector.bn_aggr(aggr[:, k - 4, :], stats[:, k - 4, :]).then_inc(epi, 1)
                elif k == 8:
                    dve.wait_ge(epi, epi_at(phase, b, at + 8))
                    nc.vector.tensor_scalar(ve[:, :], aggr[:, :, 1], EPS, None, ALU.add).then_inc(epi, 1)
                elif k == 9:
                    dve.wait_ge(std_done, b + (phase // 2 * NB + 1))
                    nc.vector.reciprocal(rec4[:, :], std4[:, :]).then_inc(epi, 1)
                elif k < 14:
                    dve.wait_ge(epi, epi_at(phase, b, at + k))
                    newton(k - 10, rstd[:, :], rec4[:, :], ve[:, :], tmp4[:, :]).then_inc(epi, 1)
                else:
                    t = k - 14
                    dve.wait_ge(epi, epi_at(phase, b, at + 14))
                    nc.vector.tensor_scalar(dst(t), y[:, t, :], aggr[:, t, 0:1], rstd[:, t:t + 1],
                                            ALU.subtract, ALU.mult).then_inc(epi, 1)

            def project_scale(phase, b, t, at, scale):
                dve.wait_ge(h_done, b + (phase * NB + 1))
                dve.wait_ge(epi, epi_at(phase, b, at))
                nc.vector.scalar_tensor_tensor(y[:, t, :], h_ps[:, t, :], scale[:, t:t + 1], b_sb[phase][:, :],
                                               ALU.mult, ALU.add).then_inc(epi, 1)

            def epilogue0(b, n):
                if n == 0:
                    dve.wait_ge(rs_act, b * NP + NP)
                    dve.wait_ge(rs_dve, b * NP + NP)
                    nc.vector.tensor_reduce(rs4[:, :], rparts[:, :, :], AX.X, ALU.add).then_inc(epi, 1)
                elif n == 1:
                    dve.wait_ge(epi, epi_at(0, b, 1))
                    nc.vector.tensor_copy(rsum[:, bass.ds(b * TI, TI)], rs4[:, :]).then_inc(epi, 1)
                elif n == 2:
                    nc.vector.tensor_scalar(deg4[:, :], rs4[:, :], al[:, 0:1], oma[:, 0:1], ALU.mult, ALU.add).then_inc(epi, 1)
                elif n == 3:
                    dve.wait_ge(epi, epi_at(0, b, 3))
                    nc.vector.tensor_scalar(mask4[:, :], deg4[:, :], 0.0, None, ALU.is_equal).then_inc(epi, 1)
                elif n == 4:
                    dve.wait_ge(epi, epi_at(0, b, 4))
                    nc.vector.tensor_tensor(safe4[:, :], deg4[:, :], mask4[:, :], ALU.add).then_inc(epi, 1)
                elif n == 5:
                    dve.wait_ge(epi, epi_at(0, b, 5))
                    nc.vector.reciprocal(rec4[:, :], safe4[:, :]).then_inc(epi, 1)
                elif n == 6:
                    dve.wait_ge(epi, epi_at(0, b, 6))
                    nc.vector.tensor_tensor(inv4[:, :], rec4[:, :], mask4[:, :], ALU.subtract).then_inc(epi, 1)
                elif n < 11:
                    project_scale(0, b, n - 7, 7, inv4)
                elif n == 11:
                    dve.wait_ge(epi, epi_at(0, b, 11))
                    dve.wait_ge(x_in, 16 * b + 16)
                    nc.vector.scalar_tensor_tensor(y[:, :, :], y[:, :, :], 0.0, term[:, :, :],
                                                   ALU.max, ALU.add).then_inc(epi, 1)
                else:
                    norm(0, b, n, 12, lambda t: big[0][:, bass.ds(b * TI + t, 1), :].rearrange("p a d -> p (a d)"))

            def epilogue1(b, n):
                if n == 0:
                    nc.vector.tensor_copy(d4[:, :], d_all[:, bass.ds(b * TI, TI)]).then_inc(epi, 1)
                elif n < 5:
                    project_scale(1, b, n - 1, 1, d4)
                else:
                    dve.wait_ge(epi, epi_at(1, b, 5))
                    nc.vector.scalar_tensor_tensor(y[:, :, :], y[:, :, :], 0.1, y[:, :, :], ALU.mult, ALU.max).then_inc(epi, 1)

            def epilogue2(b, n):
                if n == 0:
                    nc.vector.tensor_copy(d4[:, :], d_all[:, bass.ds(b * TI, TI)]).then_inc(epi, 1)
                elif n < 5:
                    dve.wait_ge(rows_out, 16 * b + 16 * NB)
                    project_scale(2, b, n - 1, 1, d4)
                elif n == 5:
                    dve.wait_ge(epi, epi_at(2, b, 5))
                    nc.vector.tensor_tensor(y[:, :, :], y[:, :, :], big[0][:, bass.ds(b * TI, TI), :], ALU.add).then_inc(epi, 1)
                else:
                    norm(2, b, n, 6, lambda t: y[:, t, :])

            epilogue = [epilogue0, epilogue1, epilogue2]

            def weighted(b, m):
                t, k = m // K, m % K
                if k == 0:
                    dve.wait_ge(got_in, b * (16 * K * TI) + 16 * K * (t + 1))
                if m == 0:
                    dve.wait_ge(staged, b * 2 + 2)
                    wait(dve, term_done, b + NB)
                    nc.vector.tensor_scalar(term[:, t, :], got[:, k, :], s16[:, m:m + 1], None, ALU.mult).then_inc(s_done, 1)
                elif k == 0:
                    nc.vector.tensor_scalar(term[:, t, :], got[:, k, :], s16[:, m:m + 1], None, ALU.mult).then_inc(s_done, 1)
                else:
                    dve.wait_ge(s_done, b * (TI * K) + m)
                    nc.vector.scalar_tensor_tensor(term[:, t, :], got[:, k, :], s16[:, m:m + 1], term[:, t, :],
                                                   ALU.mult, ALU.add).then_inc(s_done, 1)

            def one_block(phase, b, first=False, last=False):
                if phase == 0 and not first:
                    epilogue0(b - 1, 0)
                for p in range(NP):
                    if first:
                        split_v(phase, 2 * p)
                        split_v(phase, 2 * p + 1)
                    if not (last and p + 2 >= NP):
                        evac_lo(phase, b, p + 2)
                    if phase == 0:
                        row_sum(b, p)
                    if not first:
                        for n in range(1 if phase == 0 else 0, EPI[phase]):
                            if EPI_P[phase][n] == p:
                                epilogue[phase](b - 1, n)
                    if phase == 2:
                        for m in range(TI * K):
                            if SUM_P[m] == p:
                                weighted(b, m)

            def tail(phase):
                for n in range(EPI[phase]):
                    epilogue[phase](NB - 1, n)

            dve.wait_ge(const_in, CONSTS)
            dve.wait_ge(made, 2)
            nc.vector.tensor_scalar(oma[:, :], al[:, :], -1.0, 1.0, ALU.mult, ALU.add).then_inc(dmy, 1)
            dve.wait_ge(dmy, 1)
            nc.vector.tensor_scalar(one_less[:, :], ident[:, :], oma[:, 0:1], None, ALU.mult).then_inc(dmy, 1)
            evac_lo(0, 0, 0)
            evac_lo(0, 0, 1)
            one_block(0, 0, first=True)
            with dve.Fori(1, NB) as b:
                one_block(0, b)
            tail(0)
            dve.wait_ge(epi, epi_at(0, NB, 0))
            inverse_root(0, d_all[:, :], rsum[:, :], root[:, 0:NT], tmp[:, 0:NT]).then_inc(d_done, 1)
            dve.wait_ge(d_done, 1)
            one_block(1, 0, first=True)
            with dve.Fori(1, NB) as b:
                one_block(1, b)
            tail(1)
            for c in range(JC):
                dve.wait_ge(vhi_done, 2 * NT + c + 1)
                nc.vector.tensor_tensor(z_lo[:, c * JW:(c + 1) * JW], bigw[1][:, c * JW:(c + 1) * JW],
                                        z_hi[:, c * JW:(c + 1) * JW], ALU.subtract).then_inc(vlo_done, 1)
                if c == 0:
                    dve.wait_ge(sqh_done, 1)
                    nc.vector.scalar_tensor_tensor(sq_lo, h_ps[:, 0, :], -0.5, sq_hi,
                                                   ALU.mult, ALU.subtract).then_inc(sql_done, 1)

            def search(i, s):
                wait_apart(dve, (sc_done, i * JC + JC), (vi_saved, 2 * i - 2))
                nc.vector.max(m8[s][:, :], bigw[s]).then_inc(topk, 1)
                wait_apart(dve, (topk, i * 2 + 1))
                nc.vector.max_index(i8[s][:, :], m8[s][:, :], bigw[s]).then_inc(topk, 1)

            search(0, 0)
            search(1, 1)
            with dve.Fori(2, NT - 1, 2) as i:
                search(i, 0)
                search(i + 1, 1)
            dve.wait_ge(vi_saved, 2 * NT)
            sq_bc = sq_all[:, 0:NT].unsqueeze(2).to_broadcast([P, NT, K])
            nc.vector.scalar_tensor_tensor(dist[:, :, :], val[:, :, :], -2.0, sq_bc, ALU.mult, ALU.add).then_inc(wt, 1)
            dve.wait_ge(wt, 1)
            nc.vector.tensor_scalar(dist[:, :, :], dist[:, :, :], 0.0, 1e-10, ALU.max, ALU.add).then_inc(wt, 1)
            dve.wait_ge(wt, 2)
            flat = dist[:, :, :].rearrange("p t k -> p (t k)")
            inverse_root(1, tmp, flat, root, tmp).then_inc(wt, 1)
            dve.wait_ge(wt, 3)
            nc.vector.tensor_tensor(flat, flat, tmp, ALU.mult).then_inc(wt, 1)
            dve.wait_ge(exp_done, 1)
            nc.vector.tensor_reduce(ssum[:, :], s_w[:, :, :], AX.X, ALU.add).then_inc(wt, 1)
            dve.wait_ge(wt, 5)
            nc.vector.tensor_tensor(rsum[:, :], ssum[:, :], rsum[:, :], ALU.add).then_inc(wt, 1)
            inverse_root(2, d_all[:, :], rsum[:, :], root[:, 0:NT], tmp[:, 0:NT]).then_inc(d_done, 1)
            dve.wait_ge(d_done, 2)
            one_block(2, 0, first=True)
            with dve.Fori(1, NB - 1) as b:
                one_block(2, b)
            one_block(2, NB - 1, last=True)
            tail(2)

        @block.tensor
        def _(pe):
            def transposes(phase, b, q):
                c = (q // 2) % NC
                if q % 2 == 0:
                    pe.wait_ge(a_in[c % SLOTS], b * (16 * NC // SLOTS) + 16 * (phase * NB * NC // SLOTS + q // 2 // SLOTS + 1))
                wait(pe, lo_done, b * NP + (phase * STEPS + q - 1))
                for jj in range(2):
                    col = (q % 2 * 2 + jj) * P
                    for t in range(TI):
                        last = nc.tensor.transpose(t_ps[q % 2][:, jj, t * P:(t + 1) * P],
                                                   a_nat[c % SLOTS][:, t, col:col + P], ident[:, :])
                last.then_inc(tr_done, 1)

            def multiply(phase, b, p):
                pe.wait_ge(lo_done, b * NP + (phase * STEPS + p + 1))
                for jj in range(2):
                    j = 2 * p + jj
                    hi, lo = a_hi[p % SPLITS][:, jj, :], a_lo[p % SPLITS][:, jj, :]
                    nc.tensor.matmul(acc[:, :], v_hi[:, j, :], hi, start=j == 0, stop=False)
                    nc.tensor.matmul(acc[:, :], v_lo[:, j, :], hi, start=False, stop=False)
                    last = nc.tensor.matmul(acc[:, :], v_hi[:, j, :], lo, start=False, stop=j == NT - 1)
                last.then_inc(mm_done, 1)

            def add_term(phase, b):
                if phase == 0:
                    pe.wait_ge(x_in, 16 * b + 16)
                    pe.wait_ge(dmy, 2)
                else:
                    pe.wait_ge(s_done, b * (TI * K) + TI * K)
                for t in range(TI):
                    last = nc.tensor.matmul(acc[:, t * P:(t + 1) * P], term[:, t, :],
                                            one_less[:, :] if phase == 0 else ident[:, :], start=False, stop=False)
                last.then_inc(term_done, 1)

            def project(phase, b):
                pe.wait_ge(u_done, b + (phase * NB + 1))
                for t in range(TI):
                    last = nc.tensor.matmul(h_ps[:, t, :], u_sb[:, t * P:(t + 1) * P], w_sb[phase][:, :],
                                            start=True, stop=True)
                last.then_inc(h_done, 1)

            def transpose_z(b):
                pe.wait_ge(epi, epi_at(1, b, EPI[1]))
                for t in range(TI):
                    last = nc.tensor.transpose(zt_ps[:, t * P:(t + 1) * P], y[:, t, :], ident[:, :])
                last.then_inc(zt_done, 1)

            def one_block(phase, b, first=False, last=False):
                for p in range(NP):
                    if not (last and p + 2 >= NP):
                        transposes(phase, b, p + 2)
                    if p == 0:
                        wait(pe, u_done, b + phase * NB)
                    if first:
                        pe.wait_ge(vlo_done, V_BASE[phase] + 2 * p + 2)
                    if p == TERM_P and phase != 1:
                        add_term(phase, b)
                    multiply(phase, b, p)
                    if p == 1 and not first:
                        project(phase, b - 1)
                    if phase == 1 and p == ZT_P and not first:
                        transpose_z(b - 1)

            pe.wait_ge(const_in, CONSTS)
            pe.wait_ge(made, 2)
            nc.tensor.transpose(h_ps[:, 0, :], w0_nat, ident[:, :]).then_inc(w0_t, 1)
            pe.wait_ge(w0_done, 1)
            transposes(0, 0, 0)
            transposes(0, 0, 1)
            one_block(0, 0, first=True)
            with pe.Fori(1, NB) as b:
                one_block(0, b)
            project(0, NB - 1)
            one_block(1, 0, first=True)
            with pe.Fori(1, NB) as b:
                one_block(1, b)
            project(1, NB - 1)
            transpose_z(NB - 1)
            pe.wait_ge(sq_saved, NB + 1)
            nc.tensor.transpose(h_ps[:, 0, :], sq_all[:, :], ident[:, :]).then_inc(sqt_done, 1)

            def scores(i, s):
                pe.wait_ge(zi_done, i * 2 + 2)
                for c in range(JC):
                    wait(pe, sc_done, i * JC + (c - 1))
                    for h in range(JW // IB):
                        o = t_ps[c % 2][:, h, :]
                        n = c * (JW // IB) + h
                        hi, lo = z_hi[:, n * IB:(n + 1) * IB], z_lo[:, n * IB:(n + 1) * IB]
                        nc.tensor.matmul(o, zi_hi[s], hi, start=True, stop=False)
                        nc.tensor.matmul(o, zi_hi[s], lo, start=False, stop=False)
                        nc.tensor.matmul(o, zi_lo[s], hi, start=False, stop=False)
                        last = nc.tensor.matmul(o, pick[n], sq_rows, start=False, stop=True)
                    last.then_inc(gr_done, 1)

            pe.wait_ge(sq_in, 16)
            pe.wait_ge(picked, 1 + 3 * (NB // PB))
            pe.wait_ge(lo_done, 2 * STEPS + 2)
            scores(0, 0)
            scores(1, 1)
            with pe.Fori(2, NT - 1, 2) as i:
                scores(i, 0)
                scores(i + 1, 1)
            pe.wait_ge(sc_done, NT * JC)
            one_block(2, 0, first=True)
            with pe.Fori(1, NB - 1) as b:
                one_block(2, b)
            one_block(2, NB - 1, last=True)
            project(2, NB - 1)


_INS = ['x', 'adj', 'L0_gnn_t', 'L0_gnn_alpha', 'L0_gnn_W', 'L0_gnn_b', 'L1_gnn_W1', 'L1_gnn_b1', 'L1_gnn_W2', 'L1_gnn_b2']


def kernel(**inputs):
    import numpy as _np
    import concourse.bacc as _bacc
    from concourse import mybir as _mybir
    from concourse.bass_utils import run_bass_kernel_spmd as _run

    nc = _bacc.Bacc("TRN2", target_bir_lowering=False, num_devices=1)
    arrays, args = {}, []
    for name in _INS:
        a = _np.ascontiguousarray(inputs[name])
        arrays[f"in_{name}_dram"] = a
        args.append(nc.dram_tensor(f"in_{name}_dram", a.shape, _mybir.dt.from_np(a.dtype), kind="ExternalInput").ap())
    shape = inputs['x'].shape
    args.append(nc.dram_tensor("out_0_dram", shape, _mybir.dt.from_np(_np.dtype('float32')), kind="ExternalOutput").ap())
    bass_adj_resnorm_d2(nc, *args)
    r = _run(nc, [arrays], core_ids=[0])
    return r.results[0]["out_0_dram"]
```

```python
from contextlib import ExitStack

import concourse.bass as bass
from concourse import mybir


def bass_adj_resnorm_d2(nc: bass.Bass, x: bass.AP, adj: bass.AP, t0: bass.AP, alpha: bass.AP,
                        w0: bass.AP, b0: bass.AP, w1: bass.AP, b1: bass.AP, w2: bass.AP, b2: bass.AP,
                        out: bass.AP):
    f32, f32r, u32 = mybir.dt.float32, mybir.dt.float32r, mybir.dt.uint32
    ALU, ACT, AX = mybir.AluOpType, mybir.ActivationFunctionType, mybir.AxisListType

    P = 128
    N, F = x.shape
    NT = N // P
    IB = 512
    TI = IB // P
    NB = N // IB
    NP = NT // 2
    CW = 512
    NC = N // CW
    SLOTS = 4
    SPLITS = 4
    K = 4
    JW = 1024
    JC = N // JW
    XP = 4
    EPS = 1e-5
    STEPS = NB * NP

    EPI = [30, 6, 24]
    NORM_AT = [12, None, 6]
    EPI_BASE = [0, NB * EPI[0], NB * (EPI[0] + EPI[1])]
    V_BASE = [0, NT, 2 * NT + JC]
    TERM_P = NP - 2
    EPI_P = [[min(2 + n * 20 // EPI[phase] * NP // 32, NP - 1) for n in range(EPI[phase])] for phase in range(3)]
    SUM_P = [(2 + 7 * (m // K) + m % K) * NP // 32 for m in range(TI * K)]
    FIRST_SUM_P = [(6 + 6 * (m // K) + m % K) * NP // 32 for m in range(TI * K)]
    SQUARE_P = 24 * NP // 32
    ZT_P = 26 * NP // 32

    x1_dram = nc.dram_tensor("x1_scratch", (N, F), f32, kind="Internal").ap()
    v3_dram = nc.dram_tensor("v3_scratch", (N, F), f32, kind="Internal").ap()
    sq_dram = nc.dram_tensor("sq_scratch", (2, N), f32, kind="Internal").ap()

    def rows(t, b):
        return t[bass.ds(b * IB, IB), :].rearrange("(t p) n -> p t n", p=P)

    def wait(eng, sem, value):
        if not (isinstance(value, int) and value <= 0):
            eng.wait_ge(sem, value)

    def wait_apart(eng, *waits):
        for sem, v in waits:
            if not (isinstance(v, int) and v <= 0):
                eng.wait_ge(sem, v).then_inc(passed[eng], 1)

    def epi_at(phase, b, n):
        return b * EPI[phase] + (EPI_BASE[phase] + n)

    ctx = ExitStack()
    with ctx:
        def sb(name, shape, dt):
            return ctx.enter_context(nc.sbuf_tensor(name, shape, dt))

        def pb(name, shape, dt):
            return ctx.enter_context(nc.psum_tensor(name, shape, dt))

        def sem(name):
            return ctx.enter_context(nc.semaphore(name))

        a_nat = [sb(f"a_nat{s}", [P, TI, CW], f32) for s in range(SLOTS)]
        a_hi = [sb(f"a_hi{s}", [P, 2, IB], f32r) for s in range(SPLITS)]
        a_lo = [sb(f"a_lo{s}", [P, 2, IB], f32r) for s in range(SPLITS)]
        v_hi = sb("v_hi", [P, NT, P], f32r)
        v_lo = sb("v_lo", [P, NT, P], f32r)
        z_hi = v_hi[:, :, :].rearrange("p t n -> p (t n)")
        z_lo = v_lo[:, :, :].rearrange("p t n -> p (t n)")
        big = [sb(f"big{s}", [P, NT, P], f32) for s in range(2)]
        bigw = [t[:, :, :].rearrange("p t n -> p (t n)") for t in big]
        res = big[1][:, 0:TI, :]
        u_sb = sb("u_sb", [P, IB], f32)
        term = sb("term", [P, TI, P], f32)
        y = sb("y", [P, TI, P], f32)
        ident = sb("ident", [P, P], f32)
        consts = sb("consts", [P, 7, P], f32)
        one_less = consts[:, 4, :]
        w0_nat = y[:, 0, :]
        w_sb = [consts[:, n, :] for n in (0, 2, 5)]
        b_sb = [consts[:, n, :] for n in (1, 3, 6)]
        al = sb("al", [P, 1], f32)
        oma = sb("oma", [P, 1], f32)
        rparts = sb("rparts", [P, TI, NC], f32)
        rs4 = sb("rs4", [P, TI], f32)
        deg4 = sb("deg4", [P, TI], f32)
        mask4 = sb("mask4", [P, TI], f32)
        safe4 = sb("safe4", [P, TI], f32)
        rec4 = sb("rec4", [P, TI], f32)
        inv4 = sb("inv4", [P, TI], f32)
        d4 = sb("d4", [P, TI], f32)
        stats = sb("stats", [P, TI, 6], f32)
        aggr = sb("aggr", [P, TI, 2], f32)
        rstd = sb("rstd", [P, TI], f32)
        ve = sb("ve", [P, TI], f32)
        std4 = sb("std4", [P, TI], f32)
        tmp4 = sb("tmp4", [P, TI], f32)
        root = y[:, 0:TI // 2, :].rearrange("p t n -> p (t n)")[:, 0:NT * K]
        tmp = y[:, TI // 2:TI, :].rearrange("p t n -> p (t n)")[:, 0:NT * K]
        rsum = sb("rsum", [P, NT], f32)
        d_all = sb("d_all", [P, NT], f32)
        sq4 = sb("sq4", [P, TI], f32)
        sq_all = sb("sq_all", [P, P], f32)
        PB = 2 * IB // P
        picks = [a_hi[2 + h][:, :, :].rearrange("p a (b n) -> p (a b) n", n=P) for h in range(NB // PB)]
        pick = [picks[n // PB][:, n % PB, :] for n in range(NB)]
        zi_hi = [a_lo[2][:, 0, s * P:(s + 1) * P] for s in range(2)]
        zi_lo = [a_lo[2][:, 1, s * P:(s + 1) * P] for s in range(2)]
        sq_hi, sq_lo = a_lo[3][:, 0, 0:P], a_lo[3][:, 0, P:2 * P]
        sq_rows = a_lo[3][:, 1, :]
        m8 = [sb(f"m8_{s}", [P, 8], f32) for s in range(2)]
        i8 = [sb(f"i8_{s}", [P, 8], u32) for s in range(2)]
        idx = consts[:, 2:4, :].rearrange("p a n -> p (a n)").bitcast(u32)[:, 0:NT * K].rearrange("p (t k) -> p t k", k=K)
        s_w = consts[:, 0:2, :].rearrange("p a n -> p (a n)")[:, 0:NT * K].rearrange("p (t k) -> p t k", k=K)
        dist = [sb(f"dist{s}", [P, K], f32) for s in range(2)]
        ssum = [sb(f"ssum{s}", [P, 1], f32) for s in range(2)]
        deg2 = [sb(f"deg2_{s}", [P, 1], f32) for s in range(2)]
        d2_t = [sb(f"d2_t{s}", [P, 1], f32) for s in range(2)]
        half = sb("half", [P, K], f32)
        minus_half = sb("minus_half", [P, 1], f32)
        x1_t = [term[:, s, :] for s in range(2)]
        v3_t = [term[:, 2 + s, :] for s in range(2)]
        idx16 = sb("idx16", [P, TI * K], u32)
        s16 = sb("s16", [P, TI * K], f32)
        got = sb("got", [P, K, P], f32)

        t_ps = [pb(f"t_ps{s}", [P, 2, IB], f32) for s in range(2)]
        acc = pb("acc", [P, IB], f32)
        h_ps = pb("h_ps", [P, TI, P], f32)
        zt_ps = pb("zt_ps", [P, IB], f32)
        junk = pb("junk", [P, CW], f32)

        a_in = [sem(f"a_in{s}") for s in range(SLOTS)]
        const_in, rest_in, x_in, rows_out = sem("const_in"), sem("rest_in"), sem("x_in"), sem("rows_out")
        xn_in = [sem(f"xn_in{s}") for s in range(XP)]
        made, picked, w0_t, w0_done = sem("made"), sem("picked"), sem("w0_t"), sem("w0_done")
        tr_done, hi_done, lo_done, mm_done = sem("tr_done"), sem("hi_done"), sem("lo_done"), sem("mm_done")
        rs_act, rs_dve = sem("rs_act"), sem("rs_dve")
        u_done, h_done, epi, term_done = sem("u_done"), sem("h_done"), sem("epi"), sem("term_done")
        vhi_done, vlo_done = sem("vhi_done"), sem("vlo_done")
        zt_done, zt_saved, sq_done, sq_saved = sem("zt_done"), sem("zt_saved"), sem("sq_done"), sem("sq_saved")
        d_done, sqt_done, sqh_done, sql_done, sq_out, sq_in = (
            sem("d_done"), sem("sqt_done"), sem("sqh_done"), sem("sql_done"), sem("sq_out"), sem("sq_in"))
        zi_done, gr_done, sc_done, topk = sem("zi_done"), sem("gr_done"), sem("sc_done"), sem("topk")
        weigh_ops, exp_done, v3_done, staged, res_in = (
            sem("weigh_ops"), sem("exp_done"), sem("v3_done"), sem("staged"), sem("res_in"))
        v3_out = [sem(f"v3_out{s}") for s in range(2)]
        x1_in = [sem(f"x1_in{s}") for s in range(2)]
        got_in = sem("got_in")
        s_done, halves, d2_kept = sem("s_done"), sem("halves"), sem("d2_kept")
        dmy, std_done, root_done, chain = sem("dmy"), sem("std_done"), sem("root_done"), sem("chain")

        block = ctx.enter_context(nc.Block())

        dve_passed, pool_passed = sem("dve_passed"), sem("pool_passed")
        passed = {}

        @block.sync
        def _(sp):
            def load_a(phase, b, c):
                before = b * NP + (phase * STEPS + 2 * (c - SLOTS) + 2)
                wait(sp, tr_done, before)
                if phase == 0 or (phase == 1 and isinstance(b, int) and c < SLOTS):
                    wait(sp, rs_act, before)
                    wait(sp, rs_dve, before)
                sp.dma_start(a_nat[c % SLOTS][:, :, :],
                             rows(adj, b)[:, :, c * CW:(c + 1) * CW]).then_inc(a_in[c % SLOTS], 16)

            def load_x(b):
                wait(sp, term_done, b)
                if not (isinstance(b, int) and b == 0):
                    sp.wait_ge(epi, epi_at(0, b - 1, 12))
                sp.dma_start(term[:, :, :], rows(x, b)).then_inc(x_in, 16)

            def save_x1(b):
                sp.wait_ge(epi, epi_at(0, b, EPI[0]))
                sp.dma_start(rows(x1_dram, b), big[0][:, bass.ds(b * TI, TI), :]).then_inc(rows_out, 16)

            def load_res(b):
                if isinstance(b, int) and b == 0:
                    sp.wait_ge(topk, 2 * NT)
                else:
                    sp.wait_ge(epi, epi_at(2, b - 1, 6))
                sp.dma_start(res[:, :, :], rows(x1_dram, b)).then_inc(res_in, 16)

            def save_out(b):
                sp.wait_ge(epi, epi_at(2, b, EPI[2]))
                sp.dma_start(rows(out, b), y[:, :, :]).then_inc(rows_out, 16)

            def load_piece(n, source):
                w = NT // XP
                sp.dma_start(big[0][:, n * w:(n + 1) * w, :],
                             source[n * w * P:(n + 1) * w * P, :].rearrange("(t p) d -> p t d", p=P)).then_inc(xn_in[n], 16)

            sp.dma_start(al[:, :], alpha.partition_broadcast(P)).then_inc(const_in, 16)
            sp.dma_start(w0_nat, w0).then_inc(const_in, 16)
            load_a(0, 0, 0)
            for n in range(XP):
                load_piece(n, x)
                if n == 0:
                    for i, w in ((1, w1), (2, w2)):
                        sp.dma_start(w_sb[i][:, :], w).then_inc(rest_in, 16)
                    for i, b in enumerate((b0, b1, b2)):
                        sp.dma_start(b_sb[i][:, :], b.partition_broadcast(P)).then_inc(rest_in, 16)
                if 0 < n + 1 < SLOTS:
                    load_a(0, 0, n + 1)
            load_x(0)
            for c in range(SLOTS, NC):
                load_a(0, 0, c)
            with sp.Fori(1, NB) as b:
                for c in range(NC):
                    load_a(0, b, c)
                    if c == NC // 2:
                        load_x(b)
                    if c == NC - 1:
                        save_x1(b - 1)
            for c in range(SLOTS):
                load_a(1, 0, c)
            save_x1(NB - 1)
            for c in range(SLOTS, NC):
                load_a(1, 0, c)
            with sp.Fori(1, NB) as b:
                for c in range(NC):
                    load_a(1, b, c)
            for c in range(SLOTS + 1):
                load_a(2, 0, c)
            sp.wait_ge(sqh_done, 1)
            sp.dma_start(sq_dram[0, :].rearrange("(t p) -> t p", p=P), sq_hi[0:NT, :].bitcast(f32)).then_inc(sq_out, 16)
            sp.wait_ge(sql_done, 1)
            sp.dma_start(sq_dram[1, :].rearrange("(t p) -> t p", p=P), sq_lo[0:NT, :].bitcast(f32)).then_inc(sq_out, 16)
            sp.wait_ge(sq_out, 32)
            sp.wait_ge(picked, 1)
            sp.dma_start(sq_rows[0:2 * NB, :].bitcast(f32), sq_dram.rearrange("h (b n) -> (h b) n", n=IB)).then_inc(sq_in, 16)

            def load_x1_tile(i, s):
                wait(sp, v3_done, i - 1)
                sp.dma_start(x1_t[s], x1_dram[bass.ds(i * P, P), :]).then_inc(x1_in[s], 16)

            def save_v3_tile(i, s):
                sp.wait_ge(v3_done, i + 1)
                sp.dma_start(v3_dram[bass.ds(i * P, P), :], v3_t[s]).then_inc(v3_out[s], 16)

            sp.wait_ge(rows_out, 16 * NB)
            sp.wait_ge(term_done, NB)
            load_x1_tile(0, 0)
            load_x1_tile(1, 1)
            with sp.Fori(2, NT - 1, 2) as i:
                for s in range(2):
                    save_v3_tile(i + (s - 2), s)
                    load_x1_tile(i + s, s)
            for s in range(2):
                sp.wait_ge(v3_out[s], 16 * (NT // 2 - 1))
            sp.wait_ge(topk, 2 * (NT - 1))
            for n in range(XP - 1):
                load_piece(n, v3_dram)
            for s in range(2):
                save_v3_tile(NT - 2 + s, s)
            for s in range(2):
                sp.wait_ge(v3_out[s], 16 * (NT // 2))
            load_piece(XP - 1, v3_dram)
            load_res(0)
            for c in range(SLOTS + 1, NC):
                load_a(2, 0, c)
            with sp.Fori(1, NB) as b:
                for c in range(NC):
                    load_a(2, b, c)
                    if c == NC * 3 // 4:
                        load_res(b)
                    if c == NC - 1:
                        save_out(b - 1)
            save_out(NB - 1)
            sp.wait_ge(rows_out, 32 * NB)

        @block.gpsimd
        def _(pool):
            passed[pool] = pool_passed
            nc.gpsimd.memset(ident[:, :], 0.0).then_inc(made, 1)
            nc.gpsimd.memset(half[:, :], 0.5).then_inc(halves, 1)
            nc.gpsimd.memset(minus_half[:, :], -0.5).then_inc(halves, 1)
            nc.gpsimd.memset(sq_all[:, :], 0.0).then_inc(sq_saved, 1)
            pool.wait_ge(sq_saved, 1)
            pool.wait_ge(made, 1)
            nc.gpsimd.affine_select(out=ident[:, :], in_=ident[:, :], compare_op=ALU.not_equal, fill=1.0, base=0,
                                    pattern=[[-1, P]], channel_multiplier=1).then_inc(made, 1)

            def save_sq(b):
                pool.wait_ge(sq_done, TI * b + TI)
                nc.gpsimd.tensor_copy(sq_all[:, bass.ds(b * TI, TI)], sq4[:, :]).then_inc(sq_saved, 1)

            save_sq(0)
            with pool.Fori(1, NB) as b:
                save_sq(b)

            pool.wait_ge(mm_done, 2 * STEPS)
            nc.gpsimd.memset(sq_rows.bitcast(f32), 0.0).then_inc(picked, 1)
            for h in range(NB // PB):
                nc.gpsimd.memset(picks[h].bitcast(f32), 0.0).then_inc(picked, 1)
            for row in range(2):
                pool.wait_ge(picked, 1 + NB // PB * (1 + row))
                for h in range(NB // PB):
                    nc.gpsimd.affine_select(out=picks[h], in_=picks[h], compare_op=ALU.not_equal, fill=1.0,
                                            base=-row * NB - h * PB, pattern=[[-1, PB], [0, P]],
                                            channel_multiplier=1).then_inc(picked, 1)

            def stage(i, s):
                wait(pool, gr_done, i * JC - JC)
                nc.gpsimd.tensor_copy(zi_hi[s], z_hi[:, bass.ds(i * P, P)]).then_inc(zi_done, 1)
                nc.gpsimd.tensor_copy(zi_lo[s], z_lo[:, bass.ds(i * P, P)]).then_inc(zi_done, 1)

            def weigh(i, s):
                at = 7 * i
                wait_apart(pool, (topk, i * 2 + 2))
                nc.gpsimd.tensor_copy(idx[:, bass.ds(i, 1), :].rearrange("p a k -> p (a k)"), i8[s][:, 0:K]).then_inc(weigh_ops, 1)
                nc.gpsimd.tensor_scalar(dist[s][:, :], m8[s][:, 0:K], -2.0, None, ALU.mult).then_inc(weigh_ops, 1)
                wait_apart(pool, (weigh_ops, at + 2))
                nc.gpsimd.tensor_tensor(dist[s][:, :], dist[s][:, :], sq_all[:, bass.ds(i, 1)].to_broadcast([P, K]),
                                        ALU.add).then_inc(weigh_ops, 1)
                wait_apart(pool, (weigh_ops, at + 3))
                nc.gpsimd.tensor_scalar(dist[s][:, :], dist[s][:, :], 0.0, 1e-10, ALU.max, ALU.add).then_inc(weigh_ops, 1)
                wait_apart(pool, (weigh_ops, at + 4))
                nc.gpsimd.tensor_tensor(dist[s][:, :], dist[s][:, :], half[:, :], ALU.pow).then_inc(weigh_ops, 1)
                wait_apart(pool, (exp_done, i + 1))
                nc.gpsimd.tensor_tensor(deg2[s][:, :], ssum[s][:, :], rsum[:, bass.ds(i, 1)], ALU.add).then_inc(weigh_ops, 1)
                wait_apart(pool, (weigh_ops, at + 6))
                nc.gpsimd.tensor_tensor(d2_t[s][:, :], deg2[s][:, :], minus_half[:, :], ALU.pow).then_inc(weigh_ops, 1)
                wait_apart(pool, (weigh_ops, at + 7))
                nc.gpsimd.tensor_copy(d_all[:, bass.ds(i, 1)], d2_t[s][:, :]).then_inc(d2_kept, 1)

            pool.wait_ge(halves, 2)
            pool.wait_ge(vlo_done, 2 * NT + JC)
            stage(0, 0)
            stage(1, 1)
            with pool.Fori(2, NT - 1, 2) as i:
                for s in range(2):
                    stage(i + s, s)
                    weigh(i + (s - 2), s)
            weigh(NT - 2, 0)
            weigh(NT - 1, 1)
            for s in range(2):
                pool.wait_ge(v3_out[s], 16 * (NT // 2))

            def gather(b):
                wait(pool, s_done, b * (TI * K))
                nc.gpsimd.tensor_copy(idx16[:, :].rearrange("p (t k) -> p t k", k=K),
                                      idx[:, bass.ds(b * TI, TI), :]).then_inc(staged, 1)
                nc.gpsimd.tensor_copy(s16[:, :].rearrange("p (t k) -> p t k", k=K),
                                      s_w[:, bass.ds(b * TI, TI), :]).then_inc(staged, 1)
                wait_apart(pool, (staged, b * 2 + 2))
                for t in range(TI):
                    if t > 0:
                        wait_apart(pool, (s_done, b * (TI * K) + t * K))
                    for k in range(K):
                        n = t * K + k
                        nc.gpsimd.indirect_dma_start(
                            out=got[:, k, :], out_offset=None, in_=v3_dram[:, :],
                            in_offset=bass.IndirectOffsetOnAxis(ap=idx16[:, n:n + 1], axis=0)).then_inc(got_in, 16)

            gather(0)
            with pool.Fori(1, NB) as b:
                gather(b)

        @block.scalar
        def _(act):
            def split_v(phase, t):
                src = big[0][:, t, :]
                if phase != 1 and t % (NT // XP) == 0:
                    act.wait_ge(xn_in[t // (NT // XP)], 16 if phase == 0 else 32)
                if t == 0 and phase == 0:
                    act.wait_ge(const_in, 32)
                if t == 0 and phase == 1:
                    act.wait_ge(d_done, 1)
                scale = [al[:, 0:1], d_all[:, t:t + 1], 1.0][phase]
                nc.scalar.activation(v_hi[:, t, :], src, ACT.Copy, scale=scale).then_inc(vhi_done, 1)

            def evac_hi(phase, b, q):
                at = b * NP + (phase * STEPS + q)
                act.wait_ge(tr_done, at + 1)
                wait(act, mm_done, at - (SPLITS - 1))
                nc.scalar.activation(a_hi[q % SPLITS][:, :, :], t_ps[q % 2][:, :, :], ACT.Copy).then_inc(hi_done, 1)

            def save_u(phase, b):
                act.wait_ge(mm_done, b * NP + (phase * STEPS + NP))
                nc.scalar.activation(u_sb[:, :], acc[:, :], ACT.Copy).then_inc(u_done, 1)

            def square(b):
                act.wait_ge(epi, epi_at(1, b, EPI[1]))
                act.wait_ge(sq_saved, b + 1)
                for t in range(TI):
                    nc.scalar.activation(junk[:, t * P:(t + 1) * P], y[:, t, :], ACT.Square, accum_out=sq4[:, t:t + 1]).then_inc(sq_done, 1)

            def find_std(phase, b):
                act.wait_ge(epi, epi_at(phase, b, NORM_AT[phase] + 9))
                nc.scalar.activation(std4[:, :], ve[:, :], ACT.Sqrt).then_inc(std_done, 1)

            def find_root(ready, count, to, v):
                act.wait_ge(ready, count)
                nc.scalar.activation(to, v, ACT.Sqrt).then_inc(root_done, 1)

            def save_zt(b):
                act.wait_ge(zt_done, b + 1)
                nc.scalar.activation(bigw[1][:, bass.ds(b * IB, IB)], zt_ps[:, :], ACT.Copy).then_inc(zt_saved, 1)

            def row_sum(b, p):
                if p == 0:
                    if not (isinstance(b, int) and b == 0):
                        act.wait_ge(epi, epi_at(0, b - 1, 1))
                wait(act, rs_act, b * NP + p)
                nc.scalar.activation(junk[:, :], a_nat[(p // 2) % SLOTS][:, p % 2, :], ACT.Copy,
                                     accum_out=rparts[:, p % 2, p // 2:p // 2 + 1]).then_inc(rs_act, 1)

            def one_block(phase, b, first=False, last=False):
                if not first:
                    save_u(phase, b - 1)
                for p in range(NP):
                    if first:
                        split_v(phase, 2 * p)
                        split_v(phase, 2 * p + 1)
                    if not (last and p + 2 >= NP):
                        evac_hi(phase, b, p + 2)
                    if phase == 0:
                        row_sum(b, p)
                    if phase != 1 and not first and p == EPI_P[phase][NORM_AT[phase] + 8] + 1:
                        find_std(phase, b - 1)
                    if phase == 1 and not first:
                        if p == SQUARE_P:
                            square(b - 1)
                        if p == ZT_P + 1:
                            save_zt(b - 1)

            act.wait_ge(w0_t, 1)
            nc.scalar.activation(w_sb[0][:, :], h_ps[:, 0, :], ACT.Copy).then_inc(w0_done, 1)
            evac_hi(0, 0, 0)
            evac_hi(0, 0, 1)
            one_block(0, 0, first=True)
            with act.Fori(1, NB) as b:
                one_block(0, b)
            save_u(0, NB - 1)
            find_std(0, NB - 1)
            find_root(epi, epi_at(0, NB, 0), root[:, 0:NT], rsum[:, :])
            one_block(1, 0, first=True)
            with act.Fori(1, NB) as b:
                one_block(1, b)
            save_u(1, NB - 1)
            square(NB - 1)
            save_zt(NB - 1)
            act.wait_ge(zt_saved, NB)
            for c in range(JC):
                nc.scalar.activation(z_hi[:, c * JW:(c + 1) * JW], bigw[1][:, c * JW:(c + 1) * JW], ACT.Copy).then_inc(vhi_done, 1)
                if c == 0:
                    act.wait_ge(sqt_done, 1)
                    nc.scalar.activation(sq_hi, h_ps[:, 0, :], ACT.Copy, scale=-0.5).then_inc(sqh_done, 1)

            def weight(i, s):
                act.wait_ge(weigh_ops, 7 * i + 5)
                nc.scalar.activation(s_w[:, bass.ds(i, 1), :].rearrange("p a k -> p (a k)"), dist[s][:, :], ACT.Exp,
                                     scale=-0.5, accum_out=ssum[s][:, :]).then_inc(exp_done, 1)

            def scale_x1(i, s):
                act.wait_ge(weigh_ops, 7 * i + 7)
                act.wait_ge(x1_in[s], (i + (2 - s)) * 8)
                wait(act, v3_out[s], (i - s) * 8)
                nc.scalar.activation(v3_t[s], x1_t[s], ACT.Copy, scale=d2_t[s][:, 0:1]).then_inc(v3_done, 1)

            def evac_scores(i, s):
                for c in range(JC):
                    if c == JC // 2 and not isinstance(i, int):
                        weight(i - 2, s)
                    act.wait_ge(gr_done, i * JC + (c + 1))
                    if c == 0:
                        wait(act, topk, 2 * i - 2)
                    nc.scalar.activation(bigw[s][:, c * JW:(c + 1) * JW],
                                         t_ps[c % 2][:, :, :].rearrange("p a n -> p (a n)"), ACT.Copy).then_inc(sc_done, 1)
                if not isinstance(i, int):
                    scale_x1(i - 2, s)

            act.wait_ge(vlo_done, 2 * NT + JC)
            evac_scores(0, 0)
            evac_scores(1, 1)
            with act.Fori(2, NT - 1, 2) as i:
                evac_scores(i, 0)
                evac_scores(i + 1, 1)
            for s in range(2):
                weight(NT - 2 + s, s)
                scale_x1(NT - 2 + s, s)
            one_block(2, 0, first=True)
            with act.Fori(1, NB - 1) as b:
                one_block(2, b)
            one_block(2, NB - 1, last=True)
            save_u(2, NB - 1)
            find_std(2, NB - 1)

        @block.vector
        def _(dve):
            passed[dve] = dve_passed
            def split_v(phase, t):
                dve.wait_ge(vhi_done, V_BASE[phase] + t + 1)
                if phase == 2:
                    nc.vector.tensor_tensor(v_lo[:, t, :], big[0][:, t, :], v_hi[:, t, :], ALU.subtract).then_inc(vlo_done, 1)
                    return
                scale = al[:, 0:1] if phase == 0 else d_all[:, t:t + 1]
                nc.vector.scalar_tensor_tensor(v_lo[:, t, :], big[0][:, t, :], scale, v_hi[:, t, :],
                                               ALU.mult, ALU.subtract).then_inc(vlo_done, 1)

            def evac_lo(phase, b, q):
                dve.wait_ge(hi_done, b * NP + (phase * STEPS + q + 1))
                nc.vector.tensor_tensor(a_lo[q % SPLITS][:, :, :], t_ps[q % 2][:, :, :],
                                        a_hi[q % SPLITS][:, :, :], ALU.subtract).then_inc(lo_done, 1)

            def row_sum(b, p):
                if p == 0 and not (isinstance(b, int) and b == 0):
                    dve.wait_ge(epi, epi_at(0, b - 1, 1))
                nc.vector.tensor_reduce(rparts[:, 2 + p % 2, p // 2:p // 2 + 1], a_nat[(p // 2) % SLOTS][:, 2 + p % 2, :],
                                        AX.X, ALU.add).then_inc(rs_dve, 1)

            def newton(k, to, r, v, tmp):
                if k == 0:
                    return nc.vector.tensor_tensor(tmp, r, r, ALU.mult)
                if k == 1:
                    return nc.vector.tensor_tensor(tmp, tmp, v, ALU.mult)
                if k == 2:
                    return nc.vector.tensor_scalar(tmp, tmp, -0.5, 1.5, ALU.mult, ALU.add)
                return nc.vector.tensor_tensor(to, r, tmp, ALU.mult)

            def inverse_root(call, to, v, r, tmp):
                dve.wait_ge(root_done, call + 1)
                nc.vector.reciprocal(r, r).then_inc(chain, 1)
                for k in range(3):
                    dve.wait_ge(chain, 4 * call + k + 1)
                    newton(k, to, r, v, tmp).then_inc(chain, 1)
                dve.wait_ge(chain, 4 * call + 4)
                return newton(3, to, r, v, tmp)

            def norm(phase, b, n, at, dst):
                k = n - at
                if k < 4:
                    dve.wait_ge(epi, epi_at(phase, b, at))
                    nc.vector.bn_stats(stats[:, k, :], y[:, k, :]).then_inc(epi, 1)
                elif k < 8:
                    if k == 4:
                        wait_apart(dve, (epi, epi_at(phase, b, at + 4)))
                    nc.vector.bn_aggr(aggr[:, k - 4, :], stats[:, k - 4, :]).then_inc(epi, 1)
                elif k == 8:
                    dve.wait_ge(epi, epi_at(phase, b, at + 8))
                    nc.vector.tensor_scalar(ve[:, :], aggr[:, :, 1], EPS, None, ALU.add).then_inc(epi, 1)
                elif k == 9:
                    dve.wait_ge(std_done, b + (phase // 2 * NB + 1))
                    nc.vector.reciprocal(rec4[:, :], std4[:, :]).then_inc(epi, 1)
                elif k < 14:
                    dve.wait_ge(epi, epi_at(phase, b, at + k))
                    newton(k - 10, rstd[:, :], rec4[:, :], ve[:, :], tmp4[:, :]).then_inc(epi, 1)
                else:
                    t = k - 14
                    dve.wait_ge(epi, epi_at(phase, b, at + 14))
                    nc.vector.tensor_scalar(dst(t), y[:, t, :], aggr[:, t, 0:1], rstd[:, t:t + 1],
                                            ALU.subtract, ALU.mult).then_inc(epi, 1)

            def project_scale(phase, b, t, at, scale):
                dve.wait_ge(h_done, b + (phase * NB + 1))
                dve.wait_ge(rest_in, 16 * 5)
                dve.wait_ge(epi, epi_at(phase, b, at))
                nc.vector.scalar_tensor_tensor(y[:, t, :], h_ps[:, t, :], scale[:, t:t + 1], b_sb[phase][:, :],
                                               ALU.mult, ALU.add).then_inc(epi, 1)

            def epilogue0(b, n):
                if n == 0:
                    dve.wait_ge(rs_act, b * NP + NP)
                    dve.wait_ge(rs_dve, b * NP + NP)
                    nc.vector.tensor_reduce(rs4[:, :], rparts[:, :, :], AX.X, ALU.add).then_inc(epi, 1)
                elif n == 1:
                    dve.wait_ge(epi, epi_at(0, b, 1))
                    nc.vector.tensor_copy(rsum[:, bass.ds(b * TI, TI)], rs4[:, :]).then_inc(epi, 1)
                elif n == 2:
                    nc.vector.tensor_scalar(deg4[:, :], rs4[:, :], al[:, 0:1], oma[:, 0:1], ALU.mult, ALU.add).then_inc(epi, 1)
                elif n == 3:
                    dve.wait_ge(epi, epi_at(0, b, 3))
                    nc.vector.tensor_scalar(mask4[:, :], deg4[:, :], 0.0, None, ALU.is_equal).then_inc(epi, 1)
                elif n == 4:
                    dve.wait_ge(epi, epi_at(0, b, 4))
                    nc.vector.tensor_tensor(safe4[:, :], deg4[:, :], mask4[:, :], ALU.add).then_inc(epi, 1)
                elif n == 5:
                    dve.wait_ge(epi, epi_at(0, b, 5))
                    nc.vector.reciprocal(rec4[:, :], safe4[:, :]).then_inc(epi, 1)
                elif n == 6:
                    dve.wait_ge(epi, epi_at(0, b, 6))
                    nc.vector.tensor_tensor(inv4[:, :], rec4[:, :], mask4[:, :], ALU.subtract).then_inc(epi, 1)
                elif n < 11:
                    project_scale(0, b, n - 7, 7, inv4)
                elif n == 11:
                    dve.wait_ge(epi, epi_at(0, b, 11))
                    dve.wait_ge(x_in, 16 * b + 16)
                    nc.vector.scalar_tensor_tensor(y[:, :, :], y[:, :, :], 0.0, term[:, :, :],
                                                   ALU.max, ALU.add).then_inc(epi, 1)
                else:
                    norm(0, b, n, 12, lambda t: big[0][:, bass.ds(b * TI + t, 1), :].rearrange("p a d -> p (a d)"))

            def epilogue1(b, n):
                if n == 0:
                    nc.vector.tensor_copy(d4[:, :], d_all[:, bass.ds(b * TI, TI)]).then_inc(epi, 1)
                elif n < 5:
                    project_scale(1, b, n - 1, 1, d4)
                else:
                    dve.wait_ge(epi, epi_at(1, b, 5))
                    nc.vector.scalar_tensor_tensor(y[:, :, :], y[:, :, :], 0.1, y[:, :, :], ALU.mult, ALU.max).then_inc(epi, 1)

            def epilogue2(b, n):
                if n == 0:
                    nc.vector.tensor_copy(d4[:, :], d_all[:, bass.ds(b * TI, TI)]).then_inc(epi, 1)
                elif n < 5:
                    dve.wait_ge(rows_out, 16 * b + 16 * NB)
                    project_scale(2, b, n - 1, 1, d4)
                elif n == 5:
                    dve.wait_ge(epi, epi_at(2, b, 5))
                    dve.wait_ge(res_in, 16 * b + 16)
                    nc.vector.tensor_tensor(y[:, :, :], y[:, :, :], res[:, :, :], ALU.add).then_inc(epi, 1)
                else:
                    norm(2, b, n, 6, lambda t: y[:, t, :])

            epilogue = [epilogue0, epilogue1, epilogue2]

            def weighted(b, m):
                t, k = m // K, m % K
                if k == 0:
                    dve.wait_ge(got_in, b * (16 * K * TI) + 16 * K * (t + 1))
                if m == 0:
                    dve.wait_ge(staged, b * 2 + 2)
                    wait(dve, term_done, b + NB)
                    nc.vector.tensor_scalar(term[:, t, :], got[:, k, :], s16[:, m:m + 1], None, ALU.mult).then_inc(s_done, 1)
                elif k == 0:
                    nc.vector.tensor_scalar(term[:, t, :], got[:, k, :], s16[:, m:m + 1], None, ALU.mult).then_inc(s_done, 1)
                else:
                    dve.wait_ge(s_done, b * (TI * K) + m)
                    nc.vector.scalar_tensor_tensor(term[:, t, :], got[:, k, :], s16[:, m:m + 1], term[:, t, :],
                                                   ALU.mult, ALU.add).then_inc(s_done, 1)

            def one_block(phase, b, first=False, last=False):
                if phase == 0 and not first:
                    epilogue0(b - 1, 0)
                for p in range(NP):
                    if first:
                        split_v(phase, 2 * p)
                        split_v(phase, 2 * p + 1)
                    if not (last and p + 2 >= NP):
                        evac_lo(phase, b, p + 2)
                    if phase == 0:
                        row_sum(b, p)
                    if not first:
                        for n in range(1 if phase == 0 else 0, EPI[phase]):
                            if EPI_P[phase][n] == p:
                                epilogue[phase](b - 1, n)
                    if phase == 2:
                        for m in range(TI * K):
                            if (FIRST_SUM_P if first else SUM_P)[m] == p:
                                weighted(b, m)

            def tail(phase):
                for n in range(EPI[phase]):
                    epilogue[phase](NB - 1, n)

            dve.wait_ge(const_in, 32)
            dve.wait_ge(made, 2)
            nc.vector.tensor_scalar(oma[:, :], al[:, :], -1.0, 1.0, ALU.mult, ALU.add).then_inc(dmy, 1)
            dve.wait_ge(dmy, 1)
            nc.vector.tensor_scalar(one_less[:, :], ident[:, :], oma[:, 0:1], None, ALU.mult).then_inc(dmy, 1)
            evac_lo(0, 0, 0)
            evac_lo(0, 0, 1)
            one_block(0, 0, first=True)
            with dve.Fori(1, NB) as b:
                one_block(0, b)
            tail(0)
            dve.wait_ge(epi, epi_at(0, NB, 0))
            inverse_root(0, d_all[:, :], rsum[:, :], root[:, 0:NT], tmp[:, 0:NT]).then_inc(d_done, 1)
            dve.wait_ge(d_done, 1)
            one_block(1, 0, first=True)
            with dve.Fori(1, NB) as b:
                one_block(1, b)
            tail(1)
            for c in range(JC):
                dve.wait_ge(vhi_done, 2 * NT + c + 1)
                nc.vector.tensor_tensor(z_lo[:, c * JW:(c + 1) * JW], bigw[1][:, c * JW:(c + 1) * JW],
                                        z_hi[:, c * JW:(c + 1) * JW], ALU.subtract).then_inc(vlo_done, 1)
                if c == 0:
                    dve.wait_ge(sqh_done, 1)
                    nc.vector.scalar_tensor_tensor(sq_lo, h_ps[:, 0, :], -0.5, sq_hi,
                                                   ALU.mult, ALU.subtract).then_inc(sql_done, 1)

            def search(i, s):
                wait_apart(dve, (sc_done, i * JC + JC), (weigh_ops, i * 7 - 12))
                nc.vector.max(m8[s][:, :], bigw[s]).then_inc(topk, 1)
                wait_apart(dve, (topk, i * 2 + 1))
                nc.vector.max_index(i8[s][:, :], m8[s][:, :], bigw[s]).then_inc(topk, 1)

            search(0, 0)
            search(1, 1)
            with dve.Fori(2, NT - 1, 2) as i:
                search(i, 0)
                search(i + 1, 1)
            dve.wait_ge(d2_kept, NT)
            one_block(2, 0, first=True)
            with dve.Fori(1, NB - 1) as b:
                one_block(2, b)
            one_block(2, NB - 1, last=True)
            tail(2)

        @block.tensor
        def _(pe):
            def transposes(phase, b, q):
                c = (q // 2) % NC
                if q % 2 == 0:
                    pe.wait_ge(a_in[c % SLOTS], b * (16 * NC // SLOTS) + 16 * (phase * NB * NC // SLOTS + q // 2 // SLOTS + 1))
                wait(pe, lo_done, b * NP + (phase * STEPS + q - 1))
                for jj in range(2):
                    col = (q % 2 * 2 + jj) * P
                    for t in range(TI):
                        last = nc.tensor.transpose(t_ps[q % 2][:, jj, t * P:(t + 1) * P],
                                                   a_nat[c % SLOTS][:, t, col:col + P], ident[:, :])
                last.then_inc(tr_done, 1)

            def multiply(phase, b, p):
                pe.wait_ge(lo_done, b * NP + (phase * STEPS + p + 1))
                for jj in range(2):
                    j = 2 * p + jj
                    hi, lo = a_hi[p % SPLITS][:, jj, :], a_lo[p % SPLITS][:, jj, :]
                    nc.tensor.matmul(acc[:, :], v_hi[:, j, :], hi, start=j == 0, stop=False)
                    nc.tensor.matmul(acc[:, :], v_lo[:, j, :], hi, start=False, stop=False)
                    last = nc.tensor.matmul(acc[:, :], v_hi[:, j, :], lo, start=False, stop=j == NT - 1)
                last.then_inc(mm_done, 1)

            def add_term(phase, b):
                if phase == 0:
                    pe.wait_ge(x_in, 16 * b + 16)
                    pe.wait_ge(dmy, 2)
                else:
                    pe.wait_ge(s_done, b * (TI * K) + TI * K)
                for t in range(TI):
                    last = nc.tensor.matmul(acc[:, t * P:(t + 1) * P], term[:, t, :],
                                            one_less[:, :] if phase == 0 else ident[:, :], start=False, stop=False)
                last.then_inc(term_done, 1)

            def project(phase, b):
                pe.wait_ge(u_done, b + (phase * NB + 1))
                pe.wait_ge(rest_in, 16 * 5)
                for t in range(TI):
                    last = nc.tensor.matmul(h_ps[:, t, :], u_sb[:, t * P:(t + 1) * P], w_sb[phase][:, :],
                                            start=True, stop=True)
                last.then_inc(h_done, 1)

            def transpose_z(b):
                pe.wait_ge(epi, epi_at(1, b, EPI[1]))
                for t in range(TI):
                    last = nc.tensor.transpose(zt_ps[:, t * P:(t + 1) * P], y[:, t, :], ident[:, :])
                last.then_inc(zt_done, 1)

            def one_block(phase, b, first=False, last=False):
                for p in range(NP):
                    if not (last and p + 2 >= NP):
                        transposes(phase, b, p + 2)
                    if p == 0:
                        wait(pe, u_done, b + phase * NB)
                    if first:
                        pe.wait_ge(vlo_done, V_BASE[phase] + 2 * p + 2)
                    if p == TERM_P and phase != 1:
                        add_term(phase, b)
                    multiply(phase, b, p)
                    if p == 1 and not first:
                        project(phase, b - 1)
                    if phase == 1 and p == ZT_P and not first:
                        transpose_z(b - 1)

            pe.wait_ge(const_in, 32)
            pe.wait_ge(made, 2)
            nc.tensor.transpose(h_ps[:, 0, :], w0_nat, ident[:, :]).then_inc(w0_t, 1)
            pe.wait_ge(w0_done, 1)
            transposes(0, 0, 0)
            transposes(0, 0, 1)
            one_block(0, 0, first=True)
            with pe.Fori(1, NB) as b:
                one_block(0, b)
            project(0, NB - 1)
            one_block(1, 0, first=True)
            with pe.Fori(1, NB) as b:
                one_block(1, b)
            project(1, NB - 1)
            transpose_z(NB - 1)
            pe.wait_ge(sq_saved, NB + 1)
            nc.tensor.transpose(h_ps[:, 0, :], sq_all[:, :], ident[:, :]).then_inc(sqt_done, 1)

            def scores(i, s):
                pe.wait_ge(zi_done, i * 2 + 2)
                for c in range(JC):
                    wait(pe, sc_done, i * JC + (c - 1))
                    for h in range(JW // IB):
                        o = t_ps[c % 2][:, h, :]
                        n = c * (JW // IB) + h
                        hi, lo = z_hi[:, n * IB:(n + 1) * IB], z_lo[:, n * IB:(n + 1) * IB]
                        nc.tensor.matmul(o, zi_hi[s], hi, start=True, stop=False)
                        nc.tensor.matmul(o, zi_hi[s], lo, start=False, stop=False)
                        nc.tensor.matmul(o, zi_lo[s], hi, start=False, stop=False)
                        last = nc.tensor.matmul(o, pick[n], sq_rows, start=False, stop=True)
                    last.then_inc(gr_done, 1)

            pe.wait_ge(sq_in, 16)
            pe.wait_ge(picked, 1 + 3 * (NB // PB))
            pe.wait_ge(lo_done, 2 * STEPS + 2)
            scores(0, 0)
            scores(1, 1)
            with pe.Fori(2, NT - 1, 2) as i:
                scores(i, 0)
                scores(i + 1, 1)
            pe.wait_ge(sc_done, NT * JC)
            one_block(2, 0, first=True)
            with pe.Fori(1, NB - 1) as b:
                one_block(2, b)
            one_block(2, NB - 1, last=True)
            project(2, NB - 1)


_INS = ['x', 'adj', 'L0_gnn_t', 'L0_gnn_alpha', 'L0_gnn_W', 'L0_gnn_b', 'L1_gnn_W1', 'L1_gnn_b1', 'L1_gnn_W2', 'L1_gnn_b2']


def kernel(**inputs):
    import numpy as _np
    import concourse.bacc as _bacc
    from concourse import mybir as _mybir
    from concourse.bass_utils import run_bass_kernel_spmd as _run

    nc = _bacc.Bacc("TRN2", target_bir_lowering=False, num_devices=1)
    arrays, args = {}, []
    for name in _INS:
        a = _np.ascontiguousarray(inputs[name])
        arrays[f"in_{name}_dram"] = a
        args.append(nc.dram_tensor(f"in_{name}_dram", a.shape, _mybir.dt.from_np(a.dtype), kind="ExternalInput").ap())
    shape = inputs['x'].shape
    args.append(nc.dram_tensor("out_0_dram", shape, _mybir.dt.from_np(_np.dtype('float32')), kind="ExternalOutput").ap())
    bass_adj_resnorm_d2(nc, *args)
    r = _run(nc, [arrays], core_ids=[0])
    return r.results[0]["out_0_dram"]
```

```python
from contextlib import ExitStack

import concourse.bass as bass
from concourse import mybir


def bass_adj_resnorm_d2(nc: bass.Bass, x: bass.AP, adj: bass.AP, t0: bass.AP, alpha: bass.AP,
                        w0: bass.AP, b0: bass.AP, w1: bass.AP, b1: bass.AP, w2: bass.AP, b2: bass.AP,
                        out: bass.AP):
    f32, f32r, u32 = mybir.dt.float32, mybir.dt.float32r, mybir.dt.uint32
    ALU, ACT, AX = mybir.AluOpType, mybir.ActivationFunctionType, mybir.AxisListType

    P = 128
    N, F = x.shape
    NT = N // P
    IB = 512
    TI = IB // P
    NB = N // IB
    NP = NT // 2
    CW = 512
    NC = N // CW
    SLOTS = 4
    SPLITS = 4
    K = 4
    JW = 1024
    JC = N // JW
    XP = 4
    EPS = 1e-5
    STEPS = NB * NP

    EPI = [24, 6, 18]
    NORM_AT = [12, None, 6]
    EPI_BASE = [0, NB * EPI[0], NB * (EPI[0] + EPI[1])]
    VC = TI
    V_BASE = [0, NB, 2 * NB + JC]
    LAG = min(5, JC)
    EARLY = 2
    TERM_P = NP - 2
    EPI_P = [[min(2 + n * 20 // EPI[phase] * NP // 32, NP - 1) for n in range(EPI[phase])] for phase in range(3)]
    SUM_P = [(2 + 7 * (m // K) + m % K) * NP // 32 for m in range(TI * K)]
    FIRST_SUM_P = [(8 + 6 * (m // K) + m % K // 2) * NP // 32 for m in range(TI * K)]
    SQUARE_P = 24 * NP // 32
    ZT_P = 26 * NP // 32

    x1_dram = nc.dram_tensor("x1_scratch", (N, F), f32, kind="Internal").ap()
    v3_dram = nc.dram_tensor("v3_scratch", (N, F), f32, kind="Internal").ap()
    sq_dram = nc.dram_tensor("sq_scratch", (2, N), f32, kind="Internal").ap()

    def rows(t, b):
        return t[bass.ds(b * IB, IB), :].rearrange("(t p) n -> p t n", p=P)

    def wait(eng, sem, value):
        if not (isinstance(value, int) and value <= 0):
            eng.wait_ge(sem, value)

    def wait_apart(eng, *waits):
        for sem, v in waits:
            if not (isinstance(v, int) and v <= 0):
                eng.wait_ge(sem, v).then_inc(passed[eng], 1)

    def epi_at(phase, b, n):
        return b * EPI[phase] + (EPI_BASE[phase] + n)

    ctx = ExitStack()
    with ctx:
        def sb(name, shape, dt):
            return ctx.enter_context(nc.sbuf_tensor(name, shape, dt))

        def pb(name, shape, dt):
            return ctx.enter_context(nc.psum_tensor(name, shape, dt))

        def sem(name):
            return ctx.enter_context(nc.semaphore(name))

        a_nat = [sb(f"a_nat{s}", [P, TI, CW], f32) for s in range(SLOTS)]
        a_hi = [sb(f"a_hi{s}", [P, 2, IB], f32r) for s in range(SPLITS)]
        a_lo = [sb(f"a_lo{s}", [P, 2, IB], f32r) for s in range(SPLITS)]
        v_hi = sb("v_hi", [P, NT, P], f32r)
        v_lo = sb("v_lo", [P, NT, P], f32r)
        z_hi = v_hi[:, :, :].rearrange("p t n -> p (t n)")
        z_lo = v_lo[:, :, :].rearrange("p t n -> p (t n)")
        big = [sb(f"big{s}", [P, NT, P], f32) for s in range(2)]
        bigw = [t[:, :, :].rearrange("p t n -> p (t n)") for t in big]
        res = big[1][:, 0:TI, :]
        u_sb = sb("u_sb", [P, IB], f32)
        term = sb("term", [P, TI, P], f32)
        y = sb("y", [P, TI, P], f32)
        ident = sb("ident", [P, P], f32)
        consts = sb("consts", [P, 7, P], f32)
        one_less = consts[:, 4, :]
        w0_nat = y[:, 0, :]
        w_sb = [consts[:, n, :] for n in (0, 2, 5)]
        b_sb = [consts[:, n, :] for n in (1, 3, 6)]
        al = sb("al", [P, 1], f32)
        oma = sb("oma", [P, 1], f32)
        rparts = sb("rparts", [P, TI, NC], f32)
        rs4 = sb("rs4", [P, TI], f32)
        deg4 = sb("deg4", [P, TI], f32)
        mask4 = sb("mask4", [P, TI], f32)
        safe4 = sb("safe4", [P, TI], f32)
        rec4 = sb("rec4", [P, TI], f32)
        inv4 = sb("inv4", [P, TI], f32)
        d4 = sb("d4", [P, TI], f32)
        stats = sb("stats", [P, TI, 6], f32)
        aggr = sb("aggr", [P, TI, 2], f32)
        rstd = sb("rstd", [P, TI], f32)
        rsum = sb("rsum", [P, NT], f32)
        d_all = sb("d_all", [P, NT], f32)
        sq4 = sb("sq4", [P, TI], f32)
        sq_all = sb("sq_all", [P, P], f32)
        PB = 2 * IB // P
        picks = [a_hi[2 + h][:, :, :].rearrange("p a (b n) -> p (a b) n", n=P) for h in range(NB // PB)]
        pick = [picks[n // PB][:, n % PB, :] for n in range(NB)]
        zi_hi = [a_lo[2][:, 0, s * P:(s + 1) * P] for s in range(2)]
        zi_lo = [a_lo[2][:, 1, s * P:(s + 1) * P] for s in range(2)]
        sq_hi, sq_lo = a_lo[3][:, 0, 0:P], a_lo[3][:, 0, P:2 * P]
        sq_rows = a_lo[3][:, 1, :]
        m8 = [sb(f"m8_{s}", [P, 8], f32) for s in range(2)]
        i8 = [sb(f"i8_{s}", [P, 8], u32) for s in range(2)]
        idx = consts[:, 2:4, :].rearrange("p a n -> p (a n)").bitcast(u32)[:, 0:NT * K].rearrange("p (t k) -> p t k", k=K)
        s_w = consts[:, 0:2, :].rearrange("p a n -> p (a n)")[:, 0:NT * K].rearrange("p (t k) -> p t k", k=K)
        dist = [sb(f"dist{s}", [P, K], f32) for s in range(2)]
        ssum = [sb(f"ssum{s}", [P, 1], f32) for s in range(2)]
        deg2 = [sb(f"deg2_{s}", [P, 1], f32) for s in range(2)]
        d2_t = [sb(f"d2_t{s}", [P, 1], f32) for s in range(2)]
        half = sb("half", [P, K], f32)
        minus_half = sb("minus_half", [P, TI], f32)
        var4 = sb("var4", [P, TI], f32)
        x1_t = [term[:, s, :] for s in range(2)]
        v3_t = [term[:, 2 + s, :] for s in range(2)]
        idx16 = sb("idx16", [P, TI * K], u32)
        s16 = sb("s16", [P, TI * K], f32)
        got = sb("got", [P, K, P], f32)

        t_ps = [pb(f"t_ps{s}", [P, 2, IB], f32) for s in range(2)]
        acc = pb("acc", [P, IB], f32)
        h_ps = pb("h_ps", [P, TI, P], f32)
        zt_ps = pb("zt_ps", [P, IB], f32)
        junk = pb("junk", [P, CW], f32)

        a_in = [sem(f"a_in{s}") for s in range(SLOTS)]
        alpha_in, w0_in, weights_in = sem("alpha_in"), sem("w0_in"), sem("weights_in")
        x_in, rows_out = sem("x_in"), sem("rows_out")
        xn_in = [sem(f"xn_in{s}") for s in range(XP)]
        made, picked, w0_t, w0_done = sem("made"), sem("picked"), sem("w0_t"), sem("w0_done")
        tr_done, hi_done, lo_done, mm_done = sem("tr_done"), sem("hi_done"), sem("lo_done"), sem("mm_done")
        rs_act, rs_dve = sem("rs_act"), sem("rs_dve")
        u_done, h_done, epi, term_done = sem("u_done"), sem("h_done"), sem("epi"), sem("term_done")
        vhi_done, vlo_done = sem("vhi_done"), sem("vlo_done")
        zt_done, zt_saved, sq_done, sq_saved = sem("zt_done"), sem("zt_saved"), sem("sq_done"), sem("sq_saved")
        sqt_done, sqh_done, sql_done, sq_out, sq_in = (
            sem("sqt_done"), sem("sqh_done"), sem("sql_done"), sem("sq_out"), sem("sq_in"))
        zi_done, gr_done, sc_done, topk = sem("zi_done"), sem("gr_done"), sem("sc_done"), sem("topk")
        weigh_ops, exp_done, v3_done, staged, res_in = (
            sem("weigh_ops"), sem("exp_done"), sem("v3_done"), sem("staged"), sem("res_in"))
        v3_out = [sem(f"v3_out{s}") for s in range(2)]
        x1_in = [sem(f"x1_in{s}") for s in range(2)]
        got_in = sem("got_in")
        s_done, halves, d2_kept = sem("s_done"), sem("halves"), sem("d2_kept")
        less_made, d_done, v1_done = sem("less_made"), sem("d_done"), sem("v1_done")
        var_done, rstd_done = sem("var_done"), sem("rstd_done")

        block = ctx.enter_context(nc.Block())

        dve_passed, pool_passed = sem("dve_passed"), sem("pool_passed")
        passed = {}

        @block.sync
        def _(sp):
            def load_a(phase, b, c):
                before = b * NP + (phase * STEPS + 2 * (c - SLOTS) + 2)
                wait(sp, tr_done, before)
                if phase == 0 or (phase == 1 and isinstance(b, int) and c < SLOTS):
                    wait(sp, rs_act, before)
                    wait(sp, rs_dve, before)
                sp.dma_start(a_nat[c % SLOTS][:, :, :],
                             rows(adj, b)[:, :, c * CW:(c + 1) * CW]).then_inc(a_in[c % SLOTS], 16)

            def load_x(b):
                wait(sp, term_done, b)
                if not (isinstance(b, int) and b == 0):
                    sp.wait_ge(epi, epi_at(0, b - 1, 12))
                sp.dma_start(term[:, :, :], rows(x, b)).then_inc(x_in, 16)

            def save_x1(b):
                sp.wait_ge(epi, epi_at(0, b, EPI[0]))
                sp.dma_start(rows(x1_dram, b), big[0][:, bass.ds(b * TI, TI), :]).then_inc(rows_out, 16)

            def load_res(b):
                if isinstance(b, int) and b == 0:
                    sp.wait_ge(topk, 2 * NT)
                else:
                    sp.wait_ge(epi, epi_at(2, b - 1, 6))
                sp.dma_start(res[:, :, :], rows(x1_dram, b)).then_inc(res_in, 16)

            def save_out(b):
                sp.wait_ge(epi, epi_at(2, b, EPI[2]))
                sp.dma_start(rows(out, b), y[:, :, :]).then_inc(rows_out, 16)

            def load_piece(n, source):
                w = NT // XP
                sp.dma_start(big[0][:, n * w:(n + 1) * w, :],
                             source[n * w * P:(n + 1) * w * P, :].rearrange("(t p) d -> p t d", p=P)).then_inc(xn_in[n], 16)

            sp.dma_start(al[:, :], alpha.partition_broadcast(P)).then_inc(alpha_in, 16)
            load_a(0, 0, 0)
            for n in range(XP):
                load_piece(n, x)
                if n == 0:
                    sp.dma_start(w0_nat, w0).then_inc(w0_in, 16)
                    for i, w in ((1, w1), (2, w2)):
                        sp.dma_start(w_sb[i][:, :], w).then_inc(weights_in, 16)
                    for i, b in enumerate((b0, b1, b2)):
                        sp.dma_start(b_sb[i][:, :], b.partition_broadcast(P)).then_inc(weights_in, 16)
                if 0 < n + 1 < SLOTS:
                    load_a(0, 0, n + 1)
            load_x(0)
            for c in range(SLOTS, NC):
                load_a(0, 0, c)
            with sp.Fori(1, NB) as b:
                for c in range(NC):
                    load_a(0, b, c)
                    if c == NC // 2:
                        load_x(b)
                    if c == NC - 1:
                        save_x1(b - 1)
            for c in range(NC):
                load_a(1, 0, c)
            save_x1(NB - 1)
            with sp.Fori(1, NB) as b:
                for c in range(NC):
                    load_a(1, b, c)
            for c in range(SLOTS + 1):
                load_a(2, 0, c)
            sp.wait_ge(sqh_done, 1)
            sp.dma_start(sq_dram[0, :].rearrange("(t p) -> t p", p=P), sq_hi[0:NT, :].bitcast(f32)).then_inc(sq_out, 16)
            sp.wait_ge(sql_done, 1)
            sp.dma_start(sq_dram[1, :].rearrange("(t p) -> t p", p=P), sq_lo[0:NT, :].bitcast(f32)).then_inc(sq_out, 16)
            sp.wait_ge(sq_out, 32)
            sp.wait_ge(picked, 1)
            sp.dma_start(sq_rows[0:2 * NB, :].bitcast(f32), sq_dram.rearrange("h (b n) -> (h b) n", n=IB)).then_inc(sq_in, 16)

            def load_x1_tile(i, s):
                if not isinstance(i, int):
                    sp.wait_ge(v3_out[s], (i - s) * 8)
                sp.dma_start(x1_t[s], x1_dram[bass.ds(i * P, P), :]).then_inc(x1_in[s], 16)

            def save_v3_tile(i, s):
                sp.wait_ge(v3_done, i + 1)
                sp.dma_start(v3_dram[bass.ds(i * P, P), :], v3_t[s]).then_inc(v3_out[s], 16)

            sp.wait_ge(rows_out, 16 * NB)
            sp.wait_ge(term_done, NB)
            load_x1_tile(0, 0)
            load_x1_tile(1, 1)
            with sp.Fori(2, NT - 1, 2) as i:
                for s in range(2):
                    save_v3_tile(i + (s - 2), s)
                    load_x1_tile(i + s, s)
            for s in range(2):
                sp.wait_ge(v3_out[s], 16 * (NT // 2 - 1))
            sp.wait_ge(topk, 2 * (NT - 1))
            for n in range(XP - 1):
                load_piece(n, v3_dram)
            for s in range(2):
                save_v3_tile(NT - 2 + s, s)
            for s in range(2):
                sp.wait_ge(v3_out[s], 16 * (NT // 2))
            load_piece(XP - 1, v3_dram)
            load_res(0)
            for c in range(SLOTS + 1, NC):
                load_a(2, 0, c)
            with sp.Fori(1, NB) as b:
                for c in range(NC):
                    load_a(2, b, c)
                    if c == NC * 3 // 4:
                        load_res(b)
                    if c == NC - 1:
                        save_out(b - 1)
            save_out(NB - 1)
            sp.wait_ge(rows_out, 32 * NB)

        @block.gpsimd
        def _(pool):
            passed[pool] = pool_passed
            nc.gpsimd.memset(ident[:, :], 0.0).then_inc(made, 1)
            nc.gpsimd.memset(half[:, :], 0.5).then_inc(halves, 1)
            nc.gpsimd.memset(minus_half[:, :], -0.5).then_inc(halves, 1)
            nc.gpsimd.memset(sq_all[:, :], 0.0).then_inc(sq_saved, 1)
            pool.wait_ge(sq_saved, 1)
            pool.wait_ge(made, 1)
            nc.gpsimd.affine_select(out=ident[:, :], in_=ident[:, :], compare_op=ALU.not_equal, fill=1.0, base=0,
                                    pattern=[[-1, P]], channel_multiplier=1).then_inc(made, 1)

            def find_rstd(phase, b):
                wait_apart(pool, (epi, epi_at(phase, b, NORM_AT[phase] + 8)))
                nc.gpsimd.tensor_scalar(var4[:, :], aggr[:, :, 1], EPS, None, ALU.add).then_inc(var_done, 1)
                wait_apart(pool, (var_done, b + (phase // 2 * NB + 1)))
                nc.gpsimd.tensor_tensor(rstd[:, :], var4[:, :], minus_half[:, :], ALU.pow).then_inc(rstd_done, 1)

            def find_d(b):
                wait_apart(pool, (epi, epi_at(0, b, 2)))
                nc.gpsimd.tensor_tensor(d4[:, :], rs4[:, :], minus_half[:, :], ALU.pow).then_inc(d_done, 1)
                wait_apart(pool, (d_done, 2 * b + 1))
                nc.gpsimd.tensor_copy(d_all[:, bass.ds(b * TI, TI)], d4[:, :]).then_inc(d_done, 1)

            def scale_v1(b):
                wait_apart(pool, (rows_out, 16 * b + 16), (d_done, 2 * b + 2))
                v = big[0][:, bass.ds(b * TI, TI), :]
                nc.gpsimd.tensor_tensor(v, v, d_all[:, bass.ds(b * TI, TI)].unsqueeze(2).to_broadcast([P, TI, P]),
                                        ALU.mult).then_inc(v1_done, 1)

            pool.wait_ge(halves, 2)
            find_d(0)
            find_rstd(0, 0)
            with pool.Fori(1, NB) as b:
                find_d(b)
                find_rstd(0, b)
                scale_v1(b - 1)
            scale_v1(NB - 1)

            def save_sq(b):
                pool.wait_ge(sq_done, TI * b + TI)
                nc.gpsimd.tensor_copy(sq_all[:, bass.ds(b * TI, TI)], sq4[:, :]).then_inc(sq_saved, 1)

            save_sq(0)
            with pool.Fori(1, NB) as b:
                save_sq(b)

            pool.wait_ge(mm_done, 2 * STEPS)
            nc.gpsimd.memset(sq_rows.bitcast(f32), 0.0).then_inc(picked, 1)

            def make_picks(h):
                nc.gpsimd.memset(picks[h].bitcast(f32), 0.0).then_inc(picked, 1)
                for row in range(2):
                    pool.wait_ge(picked, 2 + 3 * h + row)
                    nc.gpsimd.affine_select(out=picks[h], in_=picks[h], compare_op=ALU.not_equal, fill=1.0,
                                            base=-row * NB - h * PB, pattern=[[-1, PB], [0, P]],
                                            channel_multiplier=1).then_inc(picked, 1)

            def stage(i, s):
                wait(pool, gr_done, i * JC - JC)
                nc.gpsimd.tensor_copy(zi_hi[s], z_hi[:, bass.ds(i * P, P)]).then_inc(zi_done, 1)
                nc.gpsimd.tensor_copy(zi_lo[s], z_lo[:, bass.ds(i * P, P)]).then_inc(zi_done, 1)

            def weigh(i, s):
                at = 7 * i
                wait_apart(pool, (topk, i * 2 + 2))
                nc.gpsimd.tensor_copy(idx[:, bass.ds(i, 1), :].rearrange("p a k -> p (a k)"), i8[s][:, 0:K]).then_inc(weigh_ops, 1)
                nc.gpsimd.tensor_scalar(dist[s][:, :], m8[s][:, 0:K], -2.0, None, ALU.mult).then_inc(weigh_ops, 1)
                wait_apart(pool, (weigh_ops, at + 2))
                nc.gpsimd.tensor_tensor(dist[s][:, :], dist[s][:, :], sq_all[:, bass.ds(i, 1)].to_broadcast([P, K]),
                                        ALU.add).then_inc(weigh_ops, 1)
                wait_apart(pool, (weigh_ops, at + 3))
                nc.gpsimd.tensor_scalar(dist[s][:, :], dist[s][:, :], 0.0, 1e-10, ALU.max, ALU.add).then_inc(weigh_ops, 1)
                wait_apart(pool, (weigh_ops, at + 4))
                nc.gpsimd.tensor_tensor(dist[s][:, :], dist[s][:, :], half[:, :], ALU.pow).then_inc(weigh_ops, 1)
                wait_apart(pool, (exp_done, i + 1))
                nc.gpsimd.tensor_tensor(deg2[s][:, :], ssum[s][:, :], rsum[:, bass.ds(i, 1)], ALU.add).then_inc(weigh_ops, 1)
                wait_apart(pool, (weigh_ops, at + 6))
                nc.gpsimd.tensor_tensor(d2_t[s][:, :], deg2[s][:, :], minus_half[:, 0:1], ALU.pow).then_inc(weigh_ops, 1)
                wait_apart(pool, (weigh_ops, at + 7))
                nc.gpsimd.tensor_copy(d_all[:, bass.ds(i, 1)], d2_t[s][:, :]).then_inc(d2_kept, 1)

            make_picks(0)
            pool.wait_ge(vlo_done, 2 * NB + 1)
            stage(0, 0)
            stage(1, 1)
            for h in range(1, NB // PB):
                make_picks(h)
            with pool.Fori(2, NT - 1, 2) as i:
                for s in range(2):
                    stage(i + s, s)
                    weigh(i + (s - 2), s)
            weigh(NT - 2, 0)
            for c in range(EARLY):
                pool.wait_ge(vhi_done, V_BASE[2] + c + 1)
                nc.gpsimd.tensor_tensor(v_lo[:, c * VC:(c + 1) * VC, :], big[0][:, c * VC:(c + 1) * VC, :],
                                        v_hi[:, c * VC:(c + 1) * VC, :], ALU.subtract).then_inc(vlo_done, 1)
            weigh(NT - 1, 1)
            for s in range(2):
                pool.wait_ge(v3_out[s], 16 * (NT // 2))

            def gather(b, norm=True):
                wait(pool, s_done, b * (TI * K))
                nc.gpsimd.tensor_copy(idx16[:, :].rearrange("p (t k) -> p t k", k=K),
                                      idx[:, bass.ds(b * TI, TI), :]).then_inc(staged, 1)
                nc.gpsimd.tensor_copy(s16[:, :].rearrange("p (t k) -> p t k", k=K),
                                      s_w[:, bass.ds(b * TI, TI), :]).then_inc(staged, 1)
                wait_apart(pool, (staged, b * 2 + 2))
                for t in range(TI):
                    if t == TI - 1 and norm:
                        find_rstd(2, b - 1)
                    if t > 0:
                        wait_apart(pool, (s_done, b * (TI * K) + t * K))
                    for k in range(K):
                        n = t * K + k
                        nc.gpsimd.indirect_dma_start(
                            out=got[:, k, :], out_offset=None, in_=v3_dram[:, :],
                            in_offset=bass.IndirectOffsetOnAxis(ap=idx16[:, n:n + 1], axis=0)).then_inc(got_in, 16)

            gather(0, norm=False)
            with pool.Fori(1, NB) as b:
                gather(b)
            find_rstd(2, NB - 1)

        @block.scalar
        def _(act):
            def split_v(phase, c):
                if phase == 1:
                    act.wait_ge(v1_done, c + 1)
                elif c * VC % (NT // XP) == 0:
                    act.wait_ge(xn_in[c * VC // (NT // XP)], 16 if phase == 0 else 32)
                nc.scalar.activation(v_hi[:, c * VC:(c + 1) * VC, :], big[0][:, c * VC:(c + 1) * VC, :], ACT.Copy,
                                     scale=al[:, 0:1] if phase == 0 else 1.0).then_inc(vhi_done, 1)

            def evac_hi(phase, b, q):
                at = b * NP + (phase * STEPS + q)
                act.wait_ge(tr_done, at + 1)
                wait(act, mm_done, at - (SPLITS - 1))
                nc.scalar.activation(a_hi[q % SPLITS][:, :, :], t_ps[q % 2][:, :, :], ACT.Copy).then_inc(hi_done, 1)

            def save_u(phase, b):
                act.wait_ge(mm_done, b * NP + (phase * STEPS + NP))
                nc.scalar.activation(u_sb[:, :], acc[:, :], ACT.Copy).then_inc(u_done, 1)

            def square(b):
                act.wait_ge(epi, epi_at(1, b, EPI[1]))
                act.wait_ge(sq_saved, b + 1)
                for t in range(TI):
                    nc.scalar.activation(junk[:, t * P:(t + 1) * P], y[:, t, :], ACT.Square, accum_out=sq4[:, t:t + 1]).then_inc(sq_done, 1)

            def save_zt(b):
                act.wait_ge(zt_done, b + 1)
                nc.scalar.activation(bigw[1][:, bass.ds(b * IB, IB)], zt_ps[:, :], ACT.Copy).then_inc(zt_saved, 1)

            def row_sum(b, p):
                if p == 0:
                    if not (isinstance(b, int) and b == 0):
                        act.wait_ge(epi, epi_at(0, b - 1, 1))
                wait(act, rs_act, b * NP + p)
                nc.scalar.activation(junk[:, :], a_nat[(p // 2) % SLOTS][:, p % 2, :], ACT.Copy,
                                     accum_out=rparts[:, p % 2, p // 2:p // 2 + 1]).then_inc(rs_act, 1)

            def one_block(phase, b, first=False, last=False):
                if not first:
                    save_u(phase, b - 1)
                elif phase == 1:
                    save_u(0, NB - 1)
                if first:
                    split_v(phase, 0)
                for p in range(NP):
                    if first and p % 2 == 0 and p // 2 + 1 < NB:
                        split_v(phase, p // 2 + 1)
                    if not (last and p + 2 >= NP):
                        evac_hi(phase, b, p + 2)
                    if phase == 0:
                        row_sum(b, p)
                    if phase == 0 and first and p == 1:
                        act.wait_ge(w0_t, 1)
                        nc.scalar.activation(w_sb[0][:, :], h_ps[:, 0, :], ACT.Copy).then_inc(w0_done, 1)
                    if phase == 2 and first and p == 1:
                        weight(NT - 1, 1)
                        scale_x1(NT - 1, 1)
                    if phase == 1 and not first:
                        if p == SQUARE_P:
                            square(b - 1)
                        if p == ZT_P + 1:
                            save_zt(b - 1)

            act.wait_ge(alpha_in, 16)
            evac_hi(0, 0, 0)
            evac_hi(0, 0, 1)
            one_block(0, 0, first=True)
            with act.Fori(1, NB) as b:
                one_block(0, b)
            one_block(1, 0, first=True)
            with act.Fori(1, NB) as b:
                one_block(1, b)
            save_u(1, NB - 1)
            square(NB - 1)
            save_zt(NB - 1)
            def weight(i, s):
                act.wait_ge(weigh_ops, 7 * i + 5)
                nc.scalar.activation(s_w[:, bass.ds(i, 1), :].rearrange("p a k -> p (a k)"), dist[s][:, :], ACT.Exp,
                                     scale=-0.5, accum_out=ssum[s][:, :]).then_inc(exp_done, 1)

            def scale_x1(i, s):
                act.wait_ge(weigh_ops, 7 * i + 7)
                act.wait_ge(x1_in[s], (i + (2 - s)) * 8)
                nc.scalar.activation(v3_t[s], x1_t[s], ACT.Copy, scale=d2_t[s][:, 0:1]).then_inc(v3_done, 1)

            def evac_columns(s, c):
                nc.scalar.activation(bigw[s][:, c * JW:(c + 1) * JW],
                                     t_ps[c % 2][:, :, :].rearrange("p a n -> p (a n)"), ACT.Copy).then_inc(sc_done, 1)

            def evac_scores(i, s):
                for c in range(JC):
                    if c == JC // 2 and not isinstance(i, int):
                        weight(i - 2, s)
                    act.wait_ge(gr_done, i * JC + (c + 1))
                    if c == 0:
                        wait(act, topk, 2 * i - 2)
                    evac_columns(s, c)
                if not isinstance(i, int):
                    scale_x1(i - 2, s)

            act.wait_ge(zt_saved, NB)
            for c in range(JC + LAG):
                if c < JC:
                    nc.scalar.activation(z_hi[:, c * JW:(c + 1) * JW], bigw[1][:, c * JW:(c + 1) * JW], ACT.Copy).then_inc(vhi_done, 1)
                if c == 0:
                    act.wait_ge(sqt_done, 1)
                    nc.scalar.activation(sq_hi, h_ps[:, 0, :], ACT.Copy, scale=-0.5).then_inc(sqh_done, 1)
                if c >= LAG:
                    act.wait_ge(gr_done, c - LAG + 1)
                    evac_columns(0, c - LAG)
            act.wait_ge(vlo_done, 2 * NB + JC)
            evac_scores(1, 1)
            with act.Fori(2, NT - 1, 2) as i:
                evac_scores(i, 0)
                evac_scores(i + 1, 1)
            weight(NT - 2, 0)
            scale_x1(NT - 2, 0)
            one_block(2, 0, first=True)
            with act.Fori(1, NB - 1) as b:
                one_block(2, b)
            one_block(2, NB - 1, last=True)
            save_u(2, NB - 1)

        @block.vector
        def _(dve):
            passed[dve] = dve_passed
            def split_v(phase, c):
                dve.wait_ge(vhi_done, V_BASE[phase] + c + 1)
                lo, v, hi = (t[:, c * VC:(c + 1) * VC, :] for t in (v_lo, big[0], v_hi))
                if phase == 0:
                    nc.vector.scalar_tensor_tensor(lo, v, al[:, 0:1], hi, ALU.mult, ALU.subtract).then_inc(vlo_done, 1)
                else:
                    nc.vector.tensor_tensor(lo, v, hi, ALU.subtract).then_inc(vlo_done, 1)

            def evac_lo(phase, b, q):
                dve.wait_ge(hi_done, b * NP + (phase * STEPS + q + 1))
                nc.vector.tensor_tensor(a_lo[q % SPLITS][:, :, :], t_ps[q % 2][:, :, :],
                                        a_hi[q % SPLITS][:, :, :], ALU.subtract).then_inc(lo_done, 1)

            def row_sum(b, p):
                if p == 0 and not (isinstance(b, int) and b == 0):
                    dve.wait_ge(epi, epi_at(0, b - 1, 1))
                nc.vector.tensor_reduce(rparts[:, 2 + p % 2, p // 2:p // 2 + 1], a_nat[(p // 2) % SLOTS][:, 2 + p % 2, :],
                                        AX.X, ALU.add).then_inc(rs_dve, 1)

            def norm(phase, b, n, at, dst):
                k = n - at
                if k < 4:
                    dve.wait_ge(epi, epi_at(phase, b, at))
                    nc.vector.bn_stats(stats[:, k, :], y[:, k, :]).then_inc(epi, 1)
                elif k < 8:
                    if k == 4:
                        wait_apart(dve, (epi, epi_at(phase, b, at + 4)))
                    nc.vector.bn_aggr(aggr[:, k - 4, :], stats[:, k - 4, :]).then_inc(epi, 1)
                else:
                    t = k - 8
                    dve.wait_ge(rstd_done, b + (phase // 2 * NB + 1))
                    nc.vector.tensor_scalar(dst(t), y[:, t, :], aggr[:, t, 0:1], rstd[:, t:t + 1],
                                            ALU.subtract, ALU.mult).then_inc(epi, 1)

            def project_scale(phase, b, t, at, scale):
                dve.wait_ge(h_done, b + (phase * NB + 1))
                dve.wait_ge(weights_in, 16 * 5)
                dve.wait_ge(epi, epi_at(phase, b, at))
                nc.vector.scalar_tensor_tensor(y[:, t, :], h_ps[:, t, :], scale[:, t:t + 1], b_sb[phase][:, :],
                                               ALU.mult, ALU.add).then_inc(epi, 1)

            def epilogue0(b, n):
                if n == 0:
                    dve.wait_ge(rs_act, b * NP + NP)
                    dve.wait_ge(rs_dve, b * NP + NP)
                    nc.vector.tensor_reduce(rs4[:, :], rparts[:, :, :], AX.X, ALU.add).then_inc(epi, 1)
                elif n == 1:
                    dve.wait_ge(epi, epi_at(0, b, 1))
                    nc.vector.tensor_copy(rsum[:, bass.ds(b * TI, TI)], rs4[:, :]).then_inc(epi, 1)
                elif n == 2:
                    nc.vector.tensor_scalar(deg4[:, :], rs4[:, :], al[:, 0:1], oma[:, 0:1], ALU.mult, ALU.add).then_inc(epi, 1)
                elif n == 3:
                    dve.wait_ge(epi, epi_at(0, b, 3))
                    nc.vector.tensor_scalar(mask4[:, :], deg4[:, :], 0.0, None, ALU.is_equal).then_inc(epi, 1)
                elif n == 4:
                    dve.wait_ge(epi, epi_at(0, b, 4))
                    nc.vector.tensor_tensor(safe4[:, :], deg4[:, :], mask4[:, :], ALU.add).then_inc(epi, 1)
                elif n == 5:
                    dve.wait_ge(epi, epi_at(0, b, 5))
                    nc.vector.reciprocal(rec4[:, :], safe4[:, :]).then_inc(epi, 1)
                elif n == 6:
                    dve.wait_ge(epi, epi_at(0, b, 6))
                    nc.vector.tensor_tensor(inv4[:, :], rec4[:, :], mask4[:, :], ALU.subtract).then_inc(epi, 1)
                elif n < 11:
                    project_scale(0, b, n - 7, 7, inv4)
                elif n == 11:
                    dve.wait_ge(epi, epi_at(0, b, 11))
                    dve.wait_ge(x_in, 16 * b + 16)
                    nc.vector.scalar_tensor_tensor(y[:, :, :], y[:, :, :], 0.0, term[:, :, :],
                                                   ALU.max, ALU.add).then_inc(epi, 1)
                else:
                    norm(0, b, n, 12, lambda t: big[0][:, bass.ds(b * TI + t, 1), :].rearrange("p a d -> p (a d)"))

            def epilogue1(b, n):
                if n == 0:
                    nc.vector.tensor_copy(d4[:, :], d_all[:, bass.ds(b * TI, TI)]).then_inc(epi, 1)
                elif n < 5:
                    project_scale(1, b, n - 1, 1, d4)
                else:
                    dve.wait_ge(epi, epi_at(1, b, 5))
                    nc.vector.scalar_tensor_tensor(y[:, :, :], y[:, :, :], 0.1, y[:, :, :], ALU.mult, ALU.max).then_inc(epi, 1)

            def epilogue2(b, n):
                if n == 0:
                    nc.vector.tensor_copy(d4[:, :], d_all[:, bass.ds(b * TI, TI)]).then_inc(epi, 1)
                elif n < 5:
                    dve.wait_ge(rows_out, 16 * b + 16 * NB)
                    project_scale(2, b, n - 1, 1, d4)
                elif n == 5:
                    dve.wait_ge(epi, epi_at(2, b, 5))
                    dve.wait_ge(res_in, 16 * b + 16)
                    nc.vector.tensor_tensor(y[:, :, :], y[:, :, :], res[:, :, :], ALU.add).then_inc(epi, 1)
                else:
                    norm(2, b, n, 6, lambda t: y[:, t, :])

            epilogue = [epilogue0, epilogue1, epilogue2]

            def weighted(b, m):
                t, k = m // K, m % K
                if k == 0:
                    dve.wait_ge(got_in, b * (16 * K * TI) + 16 * K * (t + 1))
                if m == 0:
                    if isinstance(b, int) and b == 0:
                        dve.wait_ge(d2_kept, NT)
                    dve.wait_ge(staged, b * 2 + 2)
                    wait(dve, term_done, b + NB)
                    nc.vector.tensor_scalar(term[:, t, :], got[:, k, :], s16[:, m:m + 1], None, ALU.mult).then_inc(s_done, 1)
                elif k == 0:
                    nc.vector.tensor_scalar(term[:, t, :], got[:, k, :], s16[:, m:m + 1], None, ALU.mult).then_inc(s_done, 1)
                else:
                    dve.wait_ge(s_done, b * (TI * K) + m)
                    nc.vector.scalar_tensor_tensor(term[:, t, :], got[:, k, :], s16[:, m:m + 1], term[:, t, :],
                                                   ALU.mult, ALU.add).then_inc(s_done, 1)

            def one_block(phase, b, first=False, last=False):
                ep, eb = (0, NB - 1) if phase == 1 and first else (phase, b - 1)
                has_epilogue = not first or phase == 1
                if ep == 0 and has_epilogue:
                    epilogue0(eb, 0)
                if first:
                    early = EARLY if phase == 2 else 0
                    if early:
                        dve.wait_ge(vlo_done, V_BASE[2] + early)
                    else:
                        split_v(phase, 0)
                for p in range(NP):
                    if first and p % 2 == 0 and early <= p // 2 + 1 < NB:
                        split_v(phase, p // 2 + 1)
                    if not (last and p + 2 >= NP):
                        evac_lo(phase, b, p + 2)
                    if phase == 0:
                        row_sum(b, p)
                    if has_epilogue:
                        for n in range(1 if ep == 0 else 0, EPI[ep]):
                            if EPI_P[ep][n] == p:
                                epilogue[ep](eb, n)
                    if phase == 2:
                        for m in range(TI * K):
                            if (FIRST_SUM_P if first else SUM_P)[m] == p:
                                weighted(b, m)

            def tail(phase):
                for n in range(EPI[phase]):
                    epilogue[phase](NB - 1, n)

            dve.wait_ge(alpha_in, 16)
            dve.wait_ge(made, 2)
            nc.vector.tensor_scalar(oma[:, :], al[:, :], -1.0, 1.0, ALU.mult, ALU.add).then_inc(less_made, 1)
            dve.wait_ge(less_made, 1)
            nc.vector.tensor_scalar(one_less[:, :], ident[:, :], oma[:, 0:1], None, ALU.mult).then_inc(less_made, 1)
            evac_lo(0, 0, 0)
            evac_lo(0, 0, 1)
            one_block(0, 0, first=True)
            with dve.Fori(1, NB) as b:
                one_block(0, b)
            one_block(1, 0, first=True)
            with dve.Fori(1, NB) as b:
                one_block(1, b)
            tail(1)
            for c in range(JC):
                dve.wait_ge(vhi_done, 2 * NB + c + 1)
                nc.vector.tensor_tensor(z_lo[:, c * JW:(c + 1) * JW], bigw[1][:, c * JW:(c + 1) * JW],
                                        z_hi[:, c * JW:(c + 1) * JW], ALU.subtract).then_inc(vlo_done, 1)
                if c == 0:
                    dve.wait_ge(sqh_done, 1)
                    nc.vector.scalar_tensor_tensor(sq_lo, h_ps[:, 0, :], -0.5, sq_hi,
                                                   ALU.mult, ALU.subtract).then_inc(sql_done, 1)

            def search(i, s):
                wait_apart(dve, (sc_done, i * JC + JC), (weigh_ops, i * 7 - 12))
                nc.vector.max(m8[s][:, :], bigw[s]).then_inc(topk, 1)
                wait_apart(dve, (topk, i * 2 + 1))
                nc.vector.max_index(i8[s][:, :], m8[s][:, :], bigw[s]).then_inc(topk, 1)

            search(0, 0)
            search(1, 1)
            with dve.Fori(2, NT - 1, 2) as i:
                search(i, 0)
                search(i + 1, 1)
            one_block(2, 0, first=True)
            with dve.Fori(1, NB - 1) as b:
                one_block(2, b)
            one_block(2, NB - 1, last=True)
            tail(2)

        @block.tensor
        def _(pe):
            def transposes(phase, b, q):
                c = (q // 2) % NC
                if q % 2 == 0:
                    pe.wait_ge(a_in[c % SLOTS], b * (16 * NC // SLOTS) + 16 * (phase * NB * NC // SLOTS + q // 2 // SLOTS + 1))
                wait(pe, lo_done, b * NP + (phase * STEPS + q - 1))
                for jj in range(2):
                    col = (q % 2 * 2 + jj) * P
                    for t in range(TI):
                        last = nc.tensor.transpose(t_ps[q % 2][:, jj, t * P:(t + 1) * P],
                                                   a_nat[c % SLOTS][:, t, col:col + P], ident[:, :])
                last.then_inc(tr_done, 1)

            def multiply(phase, b, p):
                pe.wait_ge(lo_done, b * NP + (phase * STEPS + p + 1))
                for jj in range(2):
                    j = 2 * p + jj
                    hi, lo = a_hi[p % SPLITS][:, jj, :], a_lo[p % SPLITS][:, jj, :]
                    nc.tensor.matmul(acc[:, :], v_hi[:, j, :], hi, start=j == 0, stop=False)
                    nc.tensor.matmul(acc[:, :], v_lo[:, j, :], hi, start=False, stop=False)
                    last = nc.tensor.matmul(acc[:, :], v_hi[:, j, :], lo, start=False, stop=j == NT - 1)
                last.then_inc(mm_done, 1)

            def add_term(phase, b):
                if phase == 0:
                    pe.wait_ge(x_in, 16 * b + 16)
                    pe.wait_ge(less_made, 2)
                else:
                    pe.wait_ge(s_done, b * (TI * K) + TI * K)
                for t in range(TI):
                    last = nc.tensor.matmul(acc[:, t * P:(t + 1) * P], term[:, t, :],
                                            one_less[:, :] if phase == 0 else ident[:, :], start=False, stop=False)
                last.then_inc(term_done, 1)

            def project(phase, b):
                pe.wait_ge(u_done, b + (phase * NB + 1))
                pe.wait_ge(weights_in, 16 * 5)
                pe.wait_ge(w0_done, 1)
                for t in range(TI):
                    last = nc.tensor.matmul(h_ps[:, t, :], u_sb[:, t * P:(t + 1) * P], w_sb[phase][:, :],
                                            start=True, stop=True)
                last.then_inc(h_done, 1)

            def transpose_z(b):
                pe.wait_ge(epi, epi_at(1, b, EPI[1]))
                for t in range(TI):
                    last = nc.tensor.transpose(zt_ps[:, t * P:(t + 1) * P], y[:, t, :], ident[:, :])
                last.then_inc(zt_done, 1)

            def one_block(phase, b, first=False, last=False):
                for p in range(NP):
                    if not (last and p + 2 >= NP):
                        transposes(phase, b, p + 2)
                    if p == 0:
                        wait(pe, u_done, b + phase * NB)
                    if first and p % 2 == 0:
                        pe.wait_ge(vlo_done, V_BASE[phase] + p // 2 + 1)
                    if p == TERM_P and phase != 1:
                        add_term(phase, b)
                    multiply(phase, b, p)
                    if p == 1 and (phase == 1 or not first):
                        project(0, NB - 1) if first else project(phase, b - 1)
                    if phase == 1 and p == ZT_P and not first:
                        transpose_z(b - 1)

            pe.wait_ge(made, 2)
            transposes(0, 0, 0)
            transposes(0, 0, 1)
            pe.wait_ge(w0_in, 16)
            nc.tensor.transpose(h_ps[:, 0, :], w0_nat, ident[:, :]).then_inc(w0_t, 1)
            one_block(0, 0, first=True)
            with pe.Fori(1, NB) as b:
                one_block(0, b)
            one_block(1, 0, first=True)
            with pe.Fori(1, NB) as b:
                one_block(1, b)
            project(1, NB - 1)
            transpose_z(NB - 1)
            pe.wait_ge(sq_saved, NB + 1)
            nc.tensor.transpose(h_ps[:, 0, :], sq_all[:, :], ident[:, :]).then_inc(sqt_done, 1)

            def products(s, c):
                for h in range(JW // IB):
                    o = t_ps[c % 2][:, h, :]
                    n = c * (JW // IB) + h
                    hi, lo = z_hi[:, n * IB:(n + 1) * IB], z_lo[:, n * IB:(n + 1) * IB]
                    nc.tensor.matmul(o, zi_hi[s], hi, start=True, stop=False)
                    nc.tensor.matmul(o, zi_hi[s], lo, start=False, stop=False)
                    nc.tensor.matmul(o, zi_lo[s], hi, start=False, stop=False)

            def norms(c):
                for h in range(JW // IB):
                    last = nc.tensor.matmul(t_ps[c % 2][:, h, :], pick[c * (JW // IB) + h], sq_rows,
                                            start=False, stop=True)
                last.then_inc(gr_done, 1)

            def scores(i, s):
                pe.wait_ge(zi_done, i * 2 + 2)
                for c in range(JC):
                    wait(pe, sc_done, i * JC + (c - 1))
                    products(s, c)
                    norms(c)

            def first_scores():
                pe.wait_ge(zi_done, 2)
                pe.wait_ge(lo_done, 2 * STEPS + 2)
                for c in range(JC):
                    pe.wait_ge(vlo_done, 2 * NB + c + 1)
                    wait(pe, sc_done, c - 1)
                    products(0, c)
                    if c == 1:
                        pe.wait_ge(sq_in, 16)
                        pe.wait_ge(picked, 4)
                        norms(0)
                    if c * (JW // IB) == PB:
                        pe.wait_ge(picked, 1 + 3 * (NB // PB))
                    if c > 0:
                        norms(c)

            first_scores()
            scores(1, 1)
            with pe.Fori(2, NT - 1, 2) as i:
                scores(i, 0)
                scores(i + 1, 1)
            pe.wait_ge(sc_done, NT * JC)
            one_block(2, 0, first=True)
            with pe.Fori(1, NB - 1) as b:
                one_block(2, b)
            one_block(2, NB - 1, last=True)
            project(2, NB - 1)


_INS = ['x', 'adj', 'L0_gnn_t', 'L0_gnn_alpha', 'L0_gnn_W', 'L0_gnn_b', 'L1_gnn_W1', 'L1_gnn_b1', 'L1_gnn_W2', 'L1_gnn_b2']


def kernel(**inputs):
    import numpy as _np
    import concourse.bacc as _bacc
    from concourse import mybir as _mybir
    from concourse.bass_utils import run_bass_kernel_spmd as _run

    nc = _bacc.Bacc("TRN2", target_bir_lowering=False, num_devices=1)
    arrays, args = {}, []
    for name in _INS:
        a = _np.ascontiguousarray(inputs[name])
        arrays[f"in_{name}_dram"] = a
        args.append(nc.dram_tensor(f"in_{name}_dram", a.shape, _mybir.dt.from_np(a.dtype), kind="ExternalInput").ap())
    shape = inputs['x'].shape
    args.append(nc.dram_tensor("out_0_dram", shape, _mybir.dt.from_np(_np.dtype('float32')), kind="ExternalOutput").ap())
    bass_adj_resnorm_d2(nc, *args)
    r = _run(nc, [arrays], core_ids=[0])
    return r.results[0]["out_0_dram"]
```
